# Optimizing a Trainium2 kernel written in Bass

```python
import numpy as np
import jax
import jax.numpy as jnp

def _softmax(x, axis=-1):
    return jax.nn.softmax(x, axis=axis)

def _gelu(x):
    return jax.nn.gelu(x, approximate=True)

def _silu(x):
    return jax.nn.silu(x)

def _sigmoid(x):
    return jax.nn.sigmoid(x)

def _layernorm(x, axis=-1, eps=1e-05):
    m = jnp.mean(x, axis=axis, keepdims=True)
    v = jnp.var(x, axis=axis, keepdims=True)
    return (x - m) / jnp.sqrt(v + eps)

def _scatter_add(tgt, idx, src, axis=0):
    return tgt.at[idx].add(src)

def _segment_sum(src, seg, n):
    return jax.ops.segment_sum(src, seg, n)
kernel_name = 'mk_conv_attn_hybrid_d2_conv_nchw512_r4_dbc99f'

def setup_inputs(seed: int=0):
    np.random.seed(seed)
    _w = jnp.asarray

    def _rec_inputs():
        import jax
        import jax.numpy as jnp
        _gk = jax.random.key(seed)
        x = -0.0002091 + 1 * jax.random.normal(jax.random.fold_in(_gk, 1), (16, 128, 28, 28), jnp.float32)
        return x
    x = _rec_inputs()

    def _L0_conv_setup():
        import jax, jax.numpy as jnp
        import numpy as np
        from jax import lax
        EPS = 1e-05
        DW_THRESH = 4.0
        PW_THRESH = 0.001
        C_IN = 128
        C_OUT = 128

        def _bn(x, g, b, m, v):
            inv = g * lax.rsqrt(v + EPS)
            return x * inv[None, :, None, None] + (b - m * inv)[None, :, None, None]

        def _prune(x, thresh):
            amax = jnp.max(jnp.abs(x), axis=(2, 3), keepdims=True)
            return jnp.where(amax < thresh, jnp.zeros_like(x), x)
        key = jax.random.key(seed)
        ks = jax.random.split(key, 8)
        B, H, W = (16, 28, 28)
        x = jax.random.normal(ks[0], (B, C_IN, H, W), dtype=jnp.float32)
        dw_w = jax.random.normal(ks[1], (C_IN, 1, 3, 3), dtype=jnp.float32) * 0.1
        dw_b = jax.random.normal(ks[2], (C_IN,), dtype=jnp.float32) * 0.1
        bn1_g = jnp.ones((C_IN,), jnp.float32)
        bn1_b = jnp.zeros((C_IN,), jnp.float32)
        bn1_m = jnp.zeros((C_IN,), jnp.float32)
        bn1_v = jnp.ones((C_IN,), jnp.float32)
        pw_w = jax.random.normal(ks[3], (C_OUT, C_IN, 1, 1), dtype=jnp.float32) * 0.05
        pw_b = jax.random.normal(ks[4], (C_OUT,), dtype=jnp.float32) * 0.1
        bn2_g = jnp.ones((C_OUT,), jnp.float32)
        bn2_b = jnp.zeros((C_OUT,), jnp.float32)
        bn2_m = jnp.zeros((C_OUT,), jnp.float32)
        bn2_v = jnp.ones((C_OUT,), jnp.float32)
        return dict(x=x, dw_w=dw_w, dw_b=dw_b, bn1_g=bn1_g, bn1_b=bn1_b, bn1_m=bn1_m, bn1_v=bn1_v, pw_w=pw_w, pw_b=pw_b, bn2_g=bn2_g, bn2_b=bn2_b, bn2_m=bn2_m, bn2_v=bn2_v)
    _L0_conv_all = _L0_conv_setup()
    _L0_conv_in = {k: v for k, v in _L0_conv_all.items() if k in ('dw_w', 'dw_b', 'bn1_g', 'bn1_b', 'bn1_m', 'bn1_v', 'pw_w', 'pw_b', 'bn2_g', 'bn2_b', 'bn2_m', 'bn2_v')}
    del _L0_conv_all

    def _L1_attn_setup():
        import jax, jax.numpy as jnp
        import numpy as np
        Q_THRESH = 0.25
        K_THRESH = 0.25
        V_THRESH = 0.3
        MASK_THRESH = 0.1
        NEG_INF = -1000000000.0

        def _spike(u, threshold):
            return (u >= threshold).astype(u.dtype)
        key = jax.random.key(seed)
        k1, k2, k3, k4 = jax.random.split(key, 4)
        B, L, D = (4, 1024, 128)
        x_seq = jax.random.normal(k1, (B, L, D), dtype=jnp.float32)
        Wq = jax.random.normal(k2, (D, D), dtype=jnp.float32) / np.sqrt(D)
        Wk = jax.random.normal(k3, (D, D), dtype=jnp.float32) / np.sqrt(D)
        Wv = jax.random.normal(k4, (D, D), dtype=jnp.float32) / np.sqrt(D)
        return {'x_seq': x_seq, 'Wq': Wq, 'Wk': Wk, 'Wv': Wv}
    _L1_attn_all = _L1_attn_setup()
    _L1_attn_in = {k: v for k, v in _L1_attn_all.items() if k in ('Wq', 'Wk', 'Wv')}
    del _L1_attn_all

    def _L1_ffn_setup():
        import jax, jax.numpy as jnp
        import numpy as np
        NUM_EXPERTS = 8
        TOP_K = 2
        key = jax.random.key(seed)
        ks = jax.random.split(key, 6)
        d, h, E = (128, 512, NUM_EXPERTS)
        s = 0.02
        return {'x': jax.random.normal(ks[0], (4, 1024, d), dtype=jnp.float32), 'Wr': jax.random.normal(ks[1], (d, E), dtype=jnp.float32) * s, 'W1': jax.random.normal(ks[2], (E, d, h), dtype=jnp.float32) * s, 'b1': jax.random.normal(ks[3], (E, h), dtype=jnp.float32) * s, 'W2': jax.random.normal(ks[4], (E, h, d), dtype=jnp.float32) * s, 'b2': jax.random.normal(ks[5], (E, d), dtype=jnp.float32) * s}
    _L1_ffn_all = _L1_ffn_setup()
    _L1_ffn_in = {k: v for k, v in _L1_ffn_all.items() if k in ('Wr', 'W1', 'b1', 'W2', 'b2')}
    del _L1_ffn_all
    return {'x': x, 'L0_conv_dw_w': _L0_conv_in['dw_w'], 'L0_conv_dw_b': _L0_conv_in['dw_b'], 'L0_conv_bn1_g': _L0_conv_in['bn1_g'], 'L0_conv_bn1_b': _L0_conv_in['bn1_b'], 'L0_conv_bn1_m': _L0_conv_in['bn1_m'], 'L0_conv_bn1_v': _L0_conv_in['bn1_v'], 'L0_conv_pw_w': _L0_conv_in['pw_w'], 'L0_conv_pw_b': _L0_conv_in['pw_b'], 'L0_conv_bn2_g': _L0_conv_in['bn2_g'], 'L0_conv_bn2_b': _L0_conv_in['bn2_b'], 'L0_conv_bn2_m': _L0_conv_in['bn2_m'], 'L0_conv_bn2_v': _L0_conv_in['bn2_v'], 'L1_attn_Wq': _L1_attn_in['Wq'], 'L1_attn_Wk': _L1_attn_in['Wk'], 'L1_attn_Wv': _L1_attn_in['Wv'], 'L1_ffn_Wr': _L1_ffn_in['Wr'], 'L1_ffn_W1': _L1_ffn_in['W1'], 'L1_ffn_b1': _L1_ffn_in['b1'], 'L1_ffn_W2': _L1_ffn_in['W2'], 'L1_ffn_b2': _L1_ffn_in['b2']}

def reference(x, L0_conv_dw_w, L0_conv_dw_b, L0_conv_bn1_g, L0_conv_bn1_b, L0_conv_bn1_m, L0_conv_bn1_v, L0_conv_pw_w, L0_conv_pw_b, L0_conv_bn2_g, L0_conv_bn2_b, L0_conv_bn2_m, L0_conv_bn2_v, L1_attn_Wq, L1_attn_Wk, L1_attn_Wv, L1_ffn_Wr, L1_ffn_W1, L1_ffn_b1, L1_ffn_W2, L1_ffn_b2):
    import jax
    import jax.numpy as jnp

    def _L0_conv_ref(x, dw_w, dw_b, bn1_g, bn1_b, bn1_m, bn1_v, pw_w, pw_b, bn2_g, bn2_b, bn2_m, bn2_v):
        import jax, jax.numpy as jnp
        import numpy as np
        from jax import lax
        EPS = 1e-05
        DW_THRESH = 4.0
        PW_THRESH = 0.001
        C_IN = 128
        C_OUT = 128

        def _bn(x, g, b, m, v):
            inv = g * lax.rsqrt(v + EPS)
            return x * inv[None, :, None, None] + (b - m * inv)[None, :, None, None]

        def _prune(x, thresh):
            amax = jnp.max(jnp.abs(x), axis=(2, 3), keepdims=True)
            return jnp.where(amax < thresh, jnp.zeros_like(x), x)
        dn = ('NCHW', 'OIHW', 'NCHW')
        h = lax.conv_general_dilated(x, dw_w, window_strides=(1, 1), padding=((1, 1), (1, 1)), feature_group_count=C_IN, dimension_numbers=dn)
        h = h + dw_b[None, :, None, None]
        h = jax.nn.relu(_bn(h, bn1_g, bn1_b, bn1_m, bn1_v))
        h = _prune(h, DW_THRESH)
        h = lax.conv_general_dilated(h, pw_w, window_strides=(1, 1), padding=((0, 0), (0, 0)), dimension_numbers=dn)
        h = h + pw_b[None, :, None, None]
        h = jax.nn.relu(_bn(h, bn2_g, bn2_b, bn2_m, bn2_v))
        h = _prune(h, PW_THRESH)
        return h

    def _L1_attn_ref(x_seq, Wq, Wk, Wv):
        import jax, jax.numpy as jnp
        import numpy as np
        Q_THRESH = 0.25
        K_THRESH = 0.25
        V_THRESH = 0.3
        MASK_THRESH = 0.1
        NEG_INF = -1000000000.0

        def _spike(u, threshold):
            return (u >= threshold).astype(u.dtype)
        B, L, D = x_seq.shape
        u_q = jnp.einsum('bld,ed->ble', x_seq, Wq)
        u_k = jnp.einsum('bld,ed->ble', x_seq, Wk)
        u_v = jnp.einsum('bld,ed->ble', x_seq, Wv)
        s_q = _spike(u_q, Q_THRESH)
        s_k = _spike(u_k, K_THRESH)
        s_v = _spike(u_v, V_THRESH)
        score = jnp.einsum('bld,bmd->blm', s_q, s_k)
        causal = jnp.triu(jnp.ones((L, L), dtype=bool), k=1)
        score = jnp.where(causal, NEG_INF, score)
        router_mask = (score > MASK_THRESH).astype(x_seq.dtype)
        out_spike = jnp.einsum('blm,bmd->bld', router_mask, s_v)
        return out_spike

    def _L1_ffn_ref(x, Wr, W1, b1, W2, b2):
        import jax, jax.numpy as jnp
        import numpy as np
        NUM_EXPERTS = 8
        TOP_K = 2
        B, S, D = x.shape
        E = Wr.shape[1]
        flat = x.reshape(B * S, D)
        logits = flat @ Wr
        top_vals, top_idx = jax.lax.top_k(logits, TOP_K)
        top_w = jax.nn.softmax(top_vals, axis=-1)
        N = flat.shape[0]
        gates = jnp.zeros((N, E), dtype=flat.dtype).at[jnp.arange(N)[:, None], top_idx].add(top_w)
        out = jnp.zeros_like(flat)
        for e in range(E):
            hdn = jax.nn.gelu(flat @ W1[e] + b1[e], approximate=False)
            y = hdn @ W2[e] + b2[e]
            out = out + gates[:, e:e + 1] * y
        return out.reshape(B, S, D)

    def _gn(v, G=32, eps=1e-05):
        B_, C_, H_, W_ = v.shape
        g = v.reshape(B_, G, C_ // G, H_, W_)
        m = jnp.mean(g, axis=(2, 3, 4), keepdims=True)
        s = jnp.var(g, axis=(2, 3, 4), keepdims=True)
        return ((g - m) / jnp.sqrt(s + eps)).reshape(v.shape)

    def _ln_c(v, eps=1e-06):
        m = jnp.mean(v, axis=1, keepdims=True)
        s = jnp.var(v, axis=1, keepdims=True)
        return (v - m) / jnp.sqrt(s + eps)

    def _ln_t(v, eps=1e-05):
        m = jnp.mean(v, axis=-1, keepdims=True)
        s = jnp.var(v, axis=-1, keepdims=True)
        return (v - m) / jnp.sqrt(s + eps)

    def _to_tokens(v):
        B_, C_, H_, W_ = v.shape
        return v.reshape(B_, C_, H_ * W_).transpose(0, 2, 1)

    def _from_tokens(t, like):
        B_, C_, H_, W_ = like.shape
        return t.transpose(0, 2, 1).reshape(B_, C_, H_, W_)
    x = x + _L0_conv_ref(_gn(x), L0_conv_dw_w, L0_conv_dw_b, L0_conv_bn1_g, L0_conv_bn1_b, L0_conv_bn1_m, L0_conv_bn1_v, L0_conv_pw_w, L0_conv_pw_b, L0_conv_bn2_g, L0_conv_bn2_b, L0_conv_bn2_m, L0_conv_bn2_v)
    t = _to_tokens(x)
    t = t + _L1_attn_ref(_ln_t(t), L1_attn_Wq, L1_attn_Wk, L1_attn_Wv)
    t = t + _L1_ffn_ref(_ln_t(t), L1_ffn_Wr, L1_ffn_W1, L1_ffn_b1, L1_ffn_W2, L1_ffn_b2)
    x = _from_tokens(t, x)
    return x

_drawn_inputs = setup_inputs


def setup_inputs(seed=0):
    import zlib

    import numpy as np

    out = dict(_drawn_inputs(seed))
    spreads = {'L0_conv_bn1_g': (1.0, 0.2),
     'L0_conv_bn1_b': (0.0, 0.1),
     'L0_conv_bn1_m': (0.0, 0.1),
     'L0_conv_bn1_v': (1.0, 0.2),
     'L0_conv_bn2_g': (1.0, 0.6),
     'L0_conv_bn2_b': (0.0, 0.1),
     'L0_conv_bn2_m': (0.0, 0.1),
     'L0_conv_bn2_v': (1.0, 0.6)}
    factors = {'L1_ffn_Wr': 24.95,
     'L1_ffn_W1': 27.494,
     'L1_ffn_b1': 64.0,
     'L1_ffn_W2': 24.495,
     'L1_ffn_b2': 64.0}
    for name, (base, spread) in spreads.items():
        noise = np.random.default_rng([zlib.crc32(name.encode()), seed]).standard_normal(out[name].shape)
        drawn = base * np.exp(spread * noise) if base else spread * noise
        out[name] = jnp.asarray(drawn.astype(out[name].dtype))
    for name, factor in factors.items():
        out[name] = (out[name] * factor).astype(out[name].dtype)
    return out
```

```python
from contextlib import ExitStack

import concourse.bass as bass
from concourse import mybir

F32 = mybir.dt.float32
F16 = mybir.dt.float16
BF16 = mybir.dt.bfloat16
I32 = mybir.dt.int32
U32 = mybir.dt.uint32
ALU = mybir.AluOpType
ACT = mybir.ActivationFunctionType
AX = mybir.AxisListType

P = 128
IMAGES, SIDE = 16, 28
L = SIDE * SIDE
HALF = L // 2
TOKENS = IMAGES * L
TT, NT = 112, 7
PAD = SIDE + 2
TAPS = 9
EPS = 1e-5
GROUP = 4
DW_THRESH, PW_THRESH = 4.0, 0.001
Q_THRESH, K_THRESH, V_THRESH = 0.25, 0.25, 0.3
E, HID = 8, 512
FC = HID // P
WSCALE = 64.0
TILE = 256
REGION = TOKENS + TILE
TILES = (2 * TOKENS + E * (TILE - 1)) // TILE
LEAST_TILES = 2 * TOKENS // TILE
XROWS = E * REGION + (TILES - LEAST_TILES + 1) * TILE
ROW = 2 * P + 8
SKIP = 1.0e6
MAXT = TOKENS // TILE + 1
BANK = 512
LOOP_END = (TILES - 2) // 2
POOL_CONSTS = 23
W_LOADS = 18
SET_B2 = 2
DVE_S1, DVE_S2 = 12, 33


def build(nc, a, out):
    xs = nc.dram_tensor("dispatched_rows", (XROWS, ROW // 2), U32, kind="Internal").ap()
    ys = nc.dram_tensor("expert_rows", (2 * TOKENS, P), F32, kind="Internal").ap()
    x_img = a["x"].rearrange("b c h w -> b c (h w)")
    out_img = out.rearrange("b c h w -> b c (h w)")

    with ExitStack() as ctx:
        def sb(name, shape, dt):
            return ctx.enter_context(nc.sbuf_tensor(name, shape, dt))

        def sem(name):
            return ctx.enter_context(nc.semaphore(name))

        psum = [ctx.enter_context(nc.psum_tensor(f"pair_{n}", [P, 2 * BANK], F32)) for n in "abcd"]
        pa, pb, pc, pd = psum

        ident = sb("ident", [P, P], F32)
        ident16 = sb("ident16", [P, P], F16)
        group_avg = sb("group_avg", [P, P], F32)
        before = sb("before", [P, P], BF16)
        ones = sb("ones", [P, P], BF16)
        causal = sb("causal", [P, TT], BF16)
        w_raw = sb("w_raw", [P, 4, P], F32)
        w_t = sb("w_t", [P, 4, P], F32)
        chan = sb("chan", [P, 10], F32)
        dw_w = sb("dw_w", [P, TAPS], F32)
        tap_diag = sb("tap_diag", [P, TAPS, P], F32)
        bn = sb("bn", [P, 2, 8], F32)
        wr = sb("wr", [P, E], F32)
        wr_c = sb("wr_c", [P, E], F32)
        avg_all = sb("avg_all", [P, P], F32)
        w1 = sb("w1", [P, 2, E * HID], F16)
        w2 = sb("w2", [P, 2, E * HID], F16)
        w_stage = sb("w_stage", [P, 2, HID], F32)
        b1_raw = sb("b1_raw", [E * FC, P], F32)
        b1 = sb("b1", [P, E * FC], F32)
        b2_raw = sb("b2_raw", [1, E * P], F32)
        b2 = sb("b2", [P, E * P], F16)
        b2_tmp = sb("b2_tmp", [1, 2, E * P], F16)
        two_rows = sb("two_rows", [P, P], F16)

        xb = sb("xb", [P, 2, L], F32)
        padx = sb("padx", [P, 2, PAD, PAD], F32)
        h1 = sb("h1", [P, L], F32)
        h2 = sb("h2", [P, L], F32)
        gs = sb("gs", [P, 32], F32)
        gst = sb("gst", [P, 12], F32)
        pw_masked = sb("pw_masked", [P, P], F32)
        x1 = sb("x1", [P, 2, L], F32)
        st = sb("st", [TT, 2, NT * 6], F32)
        ln = sb("ln", [TT, 2, 8, NT], F32)
        xn = sb("xn", [TT, NT, P], F32)
        xt = sb("xt", [P, L], F32)
        xf = sb("xf", [TT, NT, P], F32)
        sq = sb("sq", [P, L], BF16)
        sk = sb("sk", [P, L], BF16)
        sv = sb("sv", [TT, NT * P], BF16)
        seen_g = sb("seen_g", [P, NT * (L + TT)], BF16)
        seen = seen_g[0:TT, :]
        t2 = sb("t2", [P, 2, L], F32)
        t2_all = sb("t2_all", [P, IMAGES * L], F32)
        rows = sb("rows", [TT, 2, NT, ROW], F16)
        pos = sb("pos", [TT, 2, NT, 2], I32)
        rt = sb("rt", [TT, 12, NT * E], F32)
        rs = sb("rs", [TT, 12, NT], F32)
        chosen = sb("chosen", [TT, (NT + 1) * E], BF16)
        base = sb("base", [P, E], F32)
        descend = sb("descend", [P, E], F32)
        token = sb("token", [TT, NT], F32)

        tcount = sb("tcount", [P, E, MAXT], F32)
        tsmall = sb("tsmall", [P, 8, E], F32)
        tbig = sb("tbig", [P, 2, TILES * E], F32)
        tcol = sb("tcol", [P, 4, TILES], F32)
        tile_no = sb("tile_no", [P, TILES], F32)
        tile_row = sb("tile_row", [P, TILES], I32)
        tile_expert = sb("tile_expert", [P, TILES], F32)
        tile_w = sb("tile_w", [P, 3, TILES], I32)
        pad_at = sb("pad_at", [P, E], I32)
        pad_rows = sb("pad_rows", [P, 2, ROW], F16)

        xr = sb("xr", [P, 2, 2, ROW], F16)
        xrt = sb("xrt", [P, 2, 4, P], F16)
        g = seen_g[:, 0:4 * FC * TILE].bitcast(F32).rearrange("p (u f k) -> p u f k", u=2, f=FC)
        ghl = sb("ghl", [P, 2, 2, FC * TILE], F16)
        y = sb("y", [P, 2, 2, P], F32)
        small = sb("small", [P, 2, 4, 2], F32)
        dest = sb("dest", [P, 2, 2], I32)

        w1_place = w1[:, :, :].rearrange("p n c -> p (n c)").bitcast(F32)
        w2_place = w2[:, :, :].rearrange("p n c -> p (n c)").bitcast(F32)
        yl = w1_place[0:TT, 0:4 * NT * P].rearrange("p (u t k d) -> p u t k d", u=2, t=NT, k=2)
        ysum = w2_place[0:TT, 0:2 * NT * P].rearrange("p (u t d) -> p u t d", u=2, t=NT)
        o = w2_place[:, 2 * NT * P:2 * NT * P + 2 * L].rearrange("p (u l) -> p u l", u=2)

        S = {n: sem(n) for n in (
            "w_loaded", "pool_const", "w_turned", "w_copied", "consts_ready", "bn_ln", "bn_rstd",
            "x_loaded_0", "x_loaded_1", "gstat_ready", "gmean_ready", "gvar_ready", "grstd_raw",
            "gnorm_ready", "xn_ready", "conv_ready", "h1_ready", "pwm_ready", "pw_ready",
            "h2_ready", "x1_ready", "dve_s1", "dve_s2", "act_chain",
            "t1_ready", "var1_ready", "rstd1_raw", "norm1_ready", "xn1_ready", "xnt_ready",
            "xt_ready", "q_ready", "k_ready", "v_ready", "sq_ready", "sk_ready", "sv_ready",
            "score_ready", "seen_ready", "tri_ready", "att_ready", "t2_ready", "t2_kept_0",
            "t2_kept_1", "t2t_ready", "logit_ready", "logit_read", "var2_ready", "rstd2_raw", "norm2_ready",
            "xn2_ready", "hi_ready", "gap_ready", "gexp_ready", "chosen_ready", "rank_ready", "rank_read",
            "rows_ready", "sent_0", "sent_1", "stage_loaded", "w_hi_ready", "w_lo_ready",
            "tables_ready", "pad_ready", "padded", "dve_tab", "dve_b", "dve_c",
            "xr_loaded_0", "xr_loaded_1", "xrt_ready", "xrt_copied", "h_ready", "g_ready",
            "g_hi_ready", "ghl_ready", "y_ready", "y_copied", "dest_ready", "stored_0", "stored_1",
            "yl_loaded_0", "yl_loaded_1", "ysum_ready", "yt_ready", "o_ready", "out_0", "out_1",
            "b2_moved", "dve_set", "gates",
        )}

        block = ctx.enter_context(nc.Block())
        PAIRS = IMAGES // 2

        def wait(eng, name, value):
            if not (isinstance(value, int) and value <= 0):
                eng.wait_ge(S[name], value)

        def images(eng, body):
            body(0, 0, 0, False)
            body(1, 0, 1, False)
            with eng.Fori(1, PAIRS - 1) as j:
                body(2 * j, j, 0, False)
                body(2 * j + 1, j, 1, False)
            body(IMAGES - 2, PAIRS - 1, 0, False)
            body(IMAGES - 1, PAIRS - 1, 1, True)

        def tiles(eng, body):
            body(0, 0, 0)
            body(1, 0, 1)
            with eng.Fori(1, LOOP_END) as n:
                body(2 * n, n, 0)
                body(2 * n + 1, n, 1)
            for t in range(2 * LOOP_END, TILES):
                body(t, t // 2, t % 2)

        @block.sync
        def _(sp):
            with nc.allow_non_contiguous_dma(reason="small parameters"):
                for n, name in enumerate(("L1_attn_Wq", "L1_attn_Wk", "L1_attn_Wv")):
                    sp.dma_start(w_raw[:, n, :], a[name]).then_inc(S["w_loaded"], 16)
                sp.dma_start(w_raw[:, 3, :], a["L0_conv_pw_w"].rearrange("o c h w -> o (c h w)")).then_inc(S["w_loaded"], 16)
                sp.dma_start(dw_w[:, :], a["L0_conv_dw_w"].rearrange("c k h w -> c (k h w)")).then_inc(S["w_loaded"], 16)
                for n, name in enumerate(("dw_b", "pw_b", "bn1_g", "bn1_b", "bn1_m", "bn1_v", "bn2_g", "bn2_b", "bn2_m", "bn2_v")):
                    sp.dma_start(chan[:, n:n + 1], a["L0_conv_" + name].rearrange("(c k) -> c k", k=1)).then_inc(S["w_loaded"], 16)
                sp.dma_start(wr[:, :], a["L1_ffn_Wr"]).then_inc(S["w_loaded"], 16)
                sp.dma_start(b1_raw[:, :], a["L1_ffn_b1"].rearrange("e (f p) -> (e f) p", p=P)).then_inc(S["w_loaded"], 16)
                sp.dma_start(b2_raw[:, :], a["L1_ffn_b2"].rearrange("(k e) d -> k (e d)", k=1)).then_inc(S["w_loaded"], 16)
            sp.dma_start(xb[:, 0, :], x_img[0]).then_inc(S["x_loaded_0"], 16)
            sp.dma_start(xb[:, 1, :], x_img[1]).then_inc(S["x_loaded_1"], 16)
            wait(sp, "dve_set", SET_B2)
            sp.dma_start(b2[0:1, :], b2_tmp[:, 0, :]).then_inc(S["b2_moved"], 16)
            sp.dma_start(b2[1:2, :], b2_tmp[:, 1, :]).then_inc(S["b2_moved"], 16)

            def body(i, j, u, last):
                if u == 0:
                    wait(sp, "w_lo_ready", 2 * j)
                    sp.dma_start(w_stage[:, 0, :], a["L1_ffn_W1"][bass.ds(j, 1)].rearrange("a d h -> d (a h)")).then_inc(S["stage_loaded"], 16)
                    sp.dma_start(w_stage[:, 1, :].rearrange("p (f d) -> p f d", f=FC),
                                 a["L1_ffn_W2"][bass.ds(j, 1)].rearrange("a (f p) d -> p (a f) d", p=P)).then_inc(S["stage_loaded"], 16)
                if not isinstance(i, int) or i + 2 < IMAGES:
                    wait(sp, "x1_ready", i + 1)
                    sp.dma_start(xb[:, u, :], x_img[bass.ds(i + 2, 1)].rearrange("a c l -> c (a l)")).then_inc(S[f"x_loaded_{u}"], 16)
                wait(sp, "t2_ready", i + 1)
                sp.dma_start(t2_all[:, bass.ds(i * L, L)], t2[:, u, :]).then_inc(S[f"t2_kept_{u}"], 16)

            images(sp, body)

            wait(sp, "sent_0", 16 * 2 * NT * PAIRS)
            wait(sp, "sent_1", 16 * 2 * NT * PAIRS)
            wait(sp, "tables_ready", 1)
            wait(sp, "pad_ready", 3)
            for e in range(E):
                at = sp.value_load(pad_at[0:1, e:e + 1], min_val=0, max_val=XROWS - TILE)
                sp.dma_start(xs[bass.ds(at, TILE), :].rearrange("(s p) c -> p s c", p=P), pad_rows[:, :, :].bitcast(U32)).then_inc(S["padded"], 16)
            spare = TILES - LEAST_TILES + 1
            for n in range(spare):
                r0 = E * REGION + n * TILE
                sp.dma_start(xs[r0:r0 + TILE, :].rearrange("(s p) c -> p s c", p=P), pad_rows[:, :, :].bitcast(U32)).then_inc(S["padded"], 16)
            wait(sp, "padded", 16 * (E + spare))

            def load_tile(t, n, u):
                row = sp.value_load(tile_row[0:1, bass.ds(t, 1)], min_val=0, max_val=XROWS - TILE)
                wait(sp, "xrt_ready", t - 1)
                wait(sp, "dest_ready", t - 1)
                sp.wait_ge(S["tables_ready"], 1)
                sp.dma_start(xr[:, u, :, :].bitcast(U32), xs[bass.ds(row, TILE), :].rearrange("(s p) c -> p s c", p=P)).then_inc(S[f"xr_loaded_{u}"], 16)

            tiles(sp, load_tile)

            wait(sp, "stored_0", 32 * ((TILES + 1) // 2))
            wait(sp, "stored_1", 32 * (TILES // 2))
            y_img = ys.rearrange("(b t p k) d -> b p t (k d)", b=IMAGES, t=NT, k=2)

            def load_y(i, j, u):
                wait(sp, "ysum_ready", i - 1)
                sp.dma_start(yl[:, u, :, :, :].rearrange("p t k d -> p t (k d)"),
                             y_img[bass.ds(i, 1)].rearrange("a p t d -> p (a t) d")).then_inc(S[f"yl_loaded_{u}"], 16)

            load_y(0, 0, 0)
            load_y(1, 0, 1)
            with sp.Fori(1, PAIRS) as j:
                load_y(2 * j, j, 0)
                load_y(2 * j + 1, j, 1)

        @block.gpsimd
        def _(pool):
            G = nc.gpsimd
            done = [0]

            def const(ins):
                done[0] += 1
                ins.then_inc(S["pool_const"], 1)

            def settle():
                pool.wait_ge(S["pool_const"], done[0])

            const(G.memset(ident[:], 0.0))
            const(G.memset(ident16[:], 0.0))
            const(G.memset(group_avg[:], 1.0 / GROUP))
            const(G.memset(before[:], 1.0))
            const(G.memset(causal[:], 1.0))
            const(G.memset(ones[:], 1.0))
            const(G.memset(avg_all[:], 1.0 / P))
            const(G.memset(padx[:], 0.0))
            const(G.memset(two_rows[:], 1.0))
            const(G.memset(b2[:], 0.0))
            const(G.memset(chosen[:], 0.0))
            const(G.iota(base[:], [[REGION, E]], base=0, channel_multiplier=0, allow_small_or_imprecise_dtypes=True))
            const(G.iota(descend[:], [[-1, E]], base=E, channel_multiplier=0, allow_small_or_imprecise_dtypes=True))
            const(G.iota(token[:], [[TT, NT]], base=0, channel_multiplier=1, allow_small_or_imprecise_dtypes=True))
            settle()
            const(G.affine_select(out=ident[:], in_=ident[:], compare_op=ALU.not_equal, fill=1.0, base=0, pattern=[[-1, P]], channel_multiplier=1))
            const(G.affine_select(out=ident16[:], in_=ident16[:], compare_op=ALU.not_equal, fill=1.0, base=0, pattern=[[-1, P]], channel_multiplier=1))
            ga = group_avg[:].rearrange("p (g r) -> p g r", r=GROUP)
            const(G.affine_select(out=ga, in_=ga, compare_op=ALU.is_ge, fill=0.0, base=0, pattern=[[-GROUP, P // GROUP], [0, GROUP]], channel_multiplier=1))
            const(G.affine_select(out=before[:], in_=before[:], compare_op=ALU.is_gt, fill=0.0, base=0, pattern=[[1, P]], channel_multiplier=-1))
            const(G.affine_select(out=causal[:], in_=causal[:], compare_op=ALU.is_ge, fill=0.0, base=0, pattern=[[1, TT]], channel_multiplier=-1))
            const(G.affine_select(out=two_rows[:], in_=two_rows[:], compare_op=ALU.is_ge, fill=0.0, base=1, pattern=[[0, P]], channel_multiplier=-1))
            settle()
            const(G.affine_select(out=ga, in_=ga, compare_op=ALU.is_ge, fill=0.0, base=GROUP - 1, pattern=[[GROUP, P // GROUP], [0, GROUP]], channel_multiplier=-1))
            const(G.iota(tile_no[:], [[1, TILES]], base=0, channel_multiplier=0, allow_small_or_imprecise_dtypes=True))
            const(G.iota(tcount[:], [[0, E], [TILE, MAXT]], base=0, channel_multiplier=0, allow_small_or_imprecise_dtypes=True))
            settle()
            assert done[0] == POOL_CONSTS, done
            G.memset(pad_rows[:], 0.0).then_inc(S["pad_ready"], 1)
            wait(pool, "pad_ready", 1)
            G.memset(pad_rows[:, :, 2 * P:2 * P + 2].bitcast(F32), SKIP).then_inc(S["pad_ready"], 1)
            wait(pool, "pad_ready", 2)
            G.memset(pad_rows[:, :, 2 * P + 2:ROW].bitcast(F32), 0.0).then_inc(S["pad_ready"], 1)
            def gate(name, value):
                pool.wait_ge(S[name], value)
                pool.sem_inc(S["gates"], 1)

            rows_end = pool.to_reg(XROWS - 1)
            table_end = pool.to_reg(2 * TOKENS - 1)

            def body(i, j, u, last):
                gate("rows_ready", i + 1)
                for t in range(NT):
                    for k in range(2):
                        pool.indirect_dma_start(
                            xs, bass.IndirectOffsetOnAxis(ap=pos[:, u, t, k:k + 1].bitcast(U32), axis=0),
                            rows[:, u, t, :].bitcast(U32), None, bounds_check=rows_end, oob_is_err=False).then_inc(S[f"sent_{u}"], 16)

            images(pool, body)

            def store_tile(t, n, u):
                gate("y_copied", t + 1)
                for s in range(2):
                    pool.indirect_dma_start(
                        ys, bass.IndirectOffsetOnAxis(ap=dest[:, u, s:s + 1].bitcast(U32), axis=0),
                        y[:, u, s, :], None, bounds_check=table_end, oob_is_err=False).then_inc(S[f"stored_{u}"], 16)

            tiles(pool, store_tile)

        @block.tensor
        def _(pe):
            T = nc.tensor
            pe.wait_ge(S["pool_const"], POOL_CONSTS)
            pe.wait_ge(S["w_loaded"], 16 * W_LOADS)
            for n in range(4):
                last = T.transpose(pa[:, n * P:(n + 1) * P], w_raw[:, n, :], ident[:])
            last.then_inc(S["w_turned"], 1)
            T.transpose(pb[:, 0:E * FC], b1_raw[:, :], ident[0:E * FC, 0:E * FC]).then_inc(S["w_turned"], 1)
            T.matmul(pc[:, 0:E], avg_all[:], wr[:], start=True, stop=True).then_inc(S["w_turned"], 1)
            pe.wait_ge(S["w_copied"], 3)

            def group_stats(n, nj, nu):
                wait(pe, "h2_ready", n)
                wait(pe, "gstat_ready", n + 1)
                T.matmul(pa[:, 0:2], group_avg[:], gs[:, 8:10], start=True, stop=True).then_inc(S["gmean_ready"], 1)

            def conv(n, nj, nu):
                wait(pe, "xn_ready", n + 1)
                for tap in range(TAPS):
                    ky, kx = tap // 3, tap % 3
                    for h in range(2):
                        last = T.matmul(pa[:, h * BANK:h * BANK + HALF], tap_diag[:, tap, :],
                                        padx[:, nu, ky + 14 * h:ky + 14 * h + 14, kx:kx + SIDE],
                                        start=(tap == 0), stop=(tap == TAPS - 1))
                last.then_inc(S["conv_ready"], 1)

            def pointwise(n):
                wait(pe, "pwm_ready", n + 1)
                wait(pe, "h1_ready", n + 1)
                for h in range(2):
                    last = T.matmul(pa[:, h * BANK:h * BANK + HALF], pw_masked[:], h1[:, h * HALF:(h + 1) * HALF], start=True, stop=True)
                last.then_inc(S["pw_ready"], 1)

            pe.wait_ge(S["consts_ready"], 1)
            group_stats(0, 0, 0)
            conv(0, 0, 0)
            pointwise(0)

            def body(i, j, u, last_image):
                n, nu = i + 1, 1 - u
                if not last_image:
                    group_stats(n, 0, nu)
                wait(pe, "logit_read", i)
                wait(pe, "x1_ready", i + 1)
                for t in range(NT):
                    last = T.transpose(pb[0:TT, t * P:(t + 1) * P], x1[:, u, t * TT:(t + 1) * TT], ident[:])
                last.then_inc(S["t1_ready"], 1)
                if not last_image:
                    conv(n, 0, nu)
                wait(pe, "rank_read", i)
                wait(pe, "xn1_ready", i + 1)
                for t in range(NT):
                    last = T.transpose(pc[:, t * P:t * P + TT], xn[:, t, :], ident[0:TT, 0:TT])
                last.then_inc(S["xnt_ready"], 1)
                wait(pe, "xt_ready", i + 1)
                wait(pe, "xn2_ready", i)
                for pair, w, name in ((pd, 0, "q_ready"), (pb, 1, "k_ready")):
                    for c0, c1 in ((0, BANK), (BANK, L)):
                        last = T.matmul(pair[:, c0:c1], w_t[:, w, :], xt[:, c0:c1], start=True, stop=True)
                    last.then_inc(S[name], 1)
                for t in range(NT):
                    last = T.matmul(pc[0:TT, t * P:(t + 1) * P], xt[:, t * TT:(t + 1) * TT], w_t[:, 2, :], start=True, stop=True)
                last.then_inc(S["v_ready"], 1)
                for t in range(NT):
                    width = L - t * TT
                    if t == 0:
                        wait(pe, "sk_ready", i + 1)
                    if t >= 2:
                        wait(pe, "seen_ready", i * NT + t - 1)
                    pair = (pd, pb)[t % 2]
                    for c0 in range(0, width, BANK):
                        c1 = min(c0 + BANK, width)
                        last = T.matmul(pair[0:TT, c0:c1], sk[:, t * TT:(t + 1) * TT], sq[:, t * TT + c0:t * TT + c1], start=True, stop=True)
                    last.then_inc(S["score_ready"], 1)
                if not last_image:
                    pointwise(n)
                wait(pe, "tri_ready", i + 1)
                wait(pe, "sv_ready", i + 1)
                for h in range(2):
                    tiles = [t for t in range(NT) if t * TT < (h + 1) * HALF]
                    for t in tiles:
                        l0 = max(t * TT, h * HALF)
                        last = T.matmul(pc[:, h * BANK + l0 - h * HALF:h * BANK + HALF], sv[:, t * P:(t + 1) * P],
                                        seen[:, t * L + l0:t * L + (h + 1) * HALF], start=(t == 0), stop=(t == tiles[-1]))
                last.then_inc(S["att_ready"], 1)
                wait(pe, "t2_ready", i + 1)
                for t in range(NT):
                    last = T.transpose(pd[0:TT, t * P:(t + 1) * P], t2[:, u, t * TT:(t + 1) * TT], ident[:])
                last.then_inc(S["t2t_ready"], 1)
                wait(pe, "seen_ready", (i + 1) * NT)
                for t in range(NT):
                    last = T.matmul(pb[0:TT, t * E:(t + 1) * E], t2[:, u, t * TT:(t + 1) * TT], wr_c[:], start=True, stop=True)
                last.then_inc(S["logit_ready"], 1)
                wait(pe, "chosen_ready", i + 1)
                T.matmul(pc[:, 0:(NT + 1) * E], before[0:TT, :], chosen[:, :], start=True, stop=False)
                for t in range(NT):
                    n_after = NT - t
                    last = T.matmul(pc[:, (t + 1) * E:(NT + 1) * E].rearrange("p (t e) -> p t e", e=E), ones[0:TT, :],
                                    chosen[:, t * E:(t + 1) * E].rearrange("p (k e) -> p k e", k=1).broadcast_to([TT, n_after, E]),
                                    start=False, stop=(t == NT - 1))
                last.then_inc(S["rank_ready"], 1)

            images(pe, body)

            turned = pa[:].bitcast(F16)
            pe.wait_ge(S["tables_ready"], 1)
            pe.wait_ge(S["b2_moved"], 32)
            pe.wait_ge(S["w_lo_ready"], 2 * E)

            def turn(t, n, u):
                wait(pe, "xrt_copied", t - 1)
                wait(pe, f"xr_loaded_{u}", 16 * n + 16)
                for part in range(2):
                    for s in range(2):
                        c0 = 2 * BANK * u + (2 * part + s) * P
                        last = T.transpose(turned[:, c0:c0 + P], xr[:, u, s, part * P:(part + 1) * P], ident16[:])
                last.then_inc(S["xrt_ready"], 1)

            def hidden(t, n, u):
                w0 = pe.value_load(tile_w[0:1, 0, bass.ds(t, 1)], min_val=0, max_val=(E - 1) * HID)
                hp = (pb, pc)[u]
                wait(pe, "g_ready", FC * (t - 1))
                wait(pe, "xrt_copied", t + 1)
                for f in range(FC):
                    for m, (wp, xp) in enumerate(((0, 0), (0, 1), (1, 0))):
                        last = T.matmul(hp[:, f * TILE:(f + 1) * TILE], w1[:, wp, bass.ds(w0 + f * P, P)],
                                        xrt[:, u, 2 * xp:2 * xp + 2, :].rearrange("p s k -> p (s k)"), start=(m == 0), stop=(m == 2))
                    last.then_inc(S["h_ready"], 1)

            def output(t, n, u):
                w0 = pe.value_load(tile_w[0:1, 0, bass.ds(t, 1)], min_val=0, max_val=(E - 1) * HID)
                c0 = pe.value_load(tile_w[0:1, 1, bass.ds(t, 1)], min_val=0, max_val=(E - 1) * P)
                wait(pe, "y_copied", t - 1)
                wait(pe, "ghl_ready", 2 * t + 2)
                for s in range(2):
                    dst = pd[:, u * BANK + s * P:u * BANK + (s + 1) * P]
                    T.matmul(dst, two_rows[:], b2[:, bass.ds(c0, P)], start=True, stop=False)
                    for f in range(FC):
                        for m, (wp, gp) in enumerate(((0, 0), (1, 0), (0, 1))):
                            last = T.matmul(dst, ghl[:, u, gp, f * TILE + s * P:f * TILE + (s + 1) * P],
                                            w2[:, wp, bass.ds(w0 + f * P, P)], start=False, stop=(f == FC - 1 and m == 2))
                last.then_inc(S["y_ready"], 1)

            turn(0, 0, 0)
            turn(1, 0, 1)
            hidden(0, 0, 0)

            def step(t, n, u):
                if not isinstance(t, int) or t + 2 < TILES:
                    turn(t + 2, n + 1, u)
                if not isinstance(t, int) or t + 1 < TILES:
                    hidden(t + 1, n + u, 1 - u)
                output(t, n, u)

            tiles(pe, step)

            def turn_sum(i, j, u):
                wait(pe, "o_ready", i - 1)
                wait(pe, "ysum_ready", i + 1)
                for t in range(NT):
                    last = T.transpose((pa, pb)[u][:, t * P:t * P + TT], ysum[:, u, t, :], ident[0:TT, 0:TT])
                last.then_inc(S["yt_ready"], 1)

            turn_sum(0, 0, 0)
            turn_sum(1, 0, 1)
            with pe.Fori(1, PAIRS) as j:
                turn_sum(2 * j, j, 0)
                turn_sum(2 * j + 1, j, 1)

        @block.scalar
        def _(act):
            A = nc.scalar
            act.wait_ge(S["pool_const"], POOL_CONSTS)

            def rsqrt_start(out_, in_, tmp, wait_name, wait_value, done_name, chain):
                wait(act, wait_name, wait_value)
                A.activation(tmp, in_, ACT.Ln).then_inc(S["act_chain"], 1)
                wait(act, "act_chain", chain)
                A.activation(out_, tmp, ACT.Exp, scale=-0.5).then_inc(S[done_name], 1)

            rsqrt_start(bn[:, :, 1], bn[:, :, 0], bn[:, :, 2], "bn_ln", 1, "bn_rstd", 1)
            halves = pa[:, :].rearrange("p (h c) -> p h c", h=2)[:, :, 0:HALF]

            def s1_rstd(n, chain):
                rsqrt_start(gs[:, 19:20], gs[:, 18:19], gs[:, 28:29], "gvar_ready", n + 1, "grstd_raw", chain)

            def s1_norm(n, nu):
                wait(act, "gnorm_ready", n + 1)
                A.activation(padx[:, nu, 1:1 + SIDE, 1:1 + SIDE], xb[:, nu, :].rearrange("p (h w) -> p h w", w=SIDE),
                             ACT.Identity, scale=gs[:, 22:23], bias=gs[:, 23:24]).then_inc(S["xn_ready"], 1)

            def s1_h1(n):
                wait(act, "pw_ready", n)
                wait(act, "conv_ready", n + 1)
                A.activation(h1[:, :].rearrange("p (h c) -> p h c", h=2), halves, ACT.Relu,
                             scale=bn[:, 0, 6:7], bias=bn[:, 0, 7:8]).then_inc(S["h1_ready"], 1)

            def s1_h2(n):
                wait(act, "x1_ready", n)
                wait(act, "pw_ready", n + 1)
                A.activation(h2[:, :].rearrange("p (h c) -> p h c", h=2), halves, ACT.Relu,
                             scale=bn[:, 1, 6:7], bias=bn[:, 1, 7:8]).then_inc(S["h2_ready"], 1)

            act.wait_ge(S["consts_ready"], 1)
            s1_rstd(0, 2)
            s1_norm(0, 0)
            s1_h1(0)
            s1_h2(0)

            def body(i, j, u, last_image):
                n, nu = i + 1, 1 - u
                rsqrt_start(ln[:, 0, 6, :], ln[:, 0, 5, :], ln[:, 0, 7, :], "var1_ready", i + 1, "rstd1_raw", 3 * i + 3)
                if not last_image:
                    s1_rstd(n, 3 * i + 4)
                wait(act, "xnt_ready", i)
                wait(act, "norm1_ready", i + 1)
                for t in range(NT):
                    last = A.activation(xn[:, t, :], pb[0:TT, t * P:(t + 1) * P], ACT.Identity,
                                        scale=ln[:, 0, 1, t:t + 1], bias=ln[:, 0, 2, t:t + 1])
                last.then_inc(S["xn1_ready"], 1)
                if not last_image:
                    s1_norm(n, nu)
                    s1_h1(n)
                for t in range(NT):
                    if t == 0:
                        wait(act, "att_ready", i)
                    wait(act, "score_ready", i * NT + t + 1)
                    A.activation(seen[:, t * L + t * TT:(t + 1) * L], (pd, pb)[t % 2][0:TT, 0:L - t * TT], ACT.Sign).then_inc(S["seen_ready"], 1)
                if not last_image:
                    s1_h2(n)
                rsqrt_start(ln[:, 1, 6, :], ln[:, 1, 5, :], ln[:, 1, 7, :], "var2_ready", i + 1, "rstd2_raw", 3 * i + (4 if last_image else 5))
                wait(act, "rows_ready", i)
                wait(act, "norm2_ready", i + 1)
                for t in range(NT):
                    last = A.activation(xf[:, t, :], pd[0:TT, t * P:(t + 1) * P], ACT.Identity,
                                        scale=ln[:, 1, 1, t:t + 1], bias=ln[:, 1, 2, t:t + 1])
                last.then_inc(S["xn2_ready"], 1)
                wait(act, f"sent_{u}", 16 * 2 * NT * j)
                wait(act, "xn2_ready", i + 1)
                A.activation(rows[:, u, :, 0:P], xf[:, :, :], ACT.Identity).then_inc(S["hi_ready"], 1)
                wait(act, "gap_ready", i + 1)
                A.activation(rs[:, 5, :], rs[:, 4, :], ACT.Exp).then_inc(S["gexp_ready"], 1)
                if u == 0:
                    wait(act, "stage_loaded", 32 * j + 32)
                    A.activation(w1[:, 0, bass.ds(j * HID, HID)], w_stage[:, 0, :], ACT.Copy, scale=WSCALE).then_inc(S["w_hi_ready"], 1)
                    A.activation(w2[:, 0, bass.ds(j * HID, HID)], w_stage[:, 1, :], ACT.Copy, scale=WSCALE).then_inc(S["w_hi_ready"], 1)

            images(act, body)

            turned = pa[:].bitcast(F16)
            act.wait_ge(S["tables_ready"], 1)

            def copy_turned(t, n, u):
                wait(act, "h_ready", FC * (t - 1))
                wait(act, "xrt_ready", t + 1)
                A.activation(xrt[:, u, :, :].rearrange("p s k -> p (s k)"), turned[:, 2 * BANK * u:2 * BANK * u + 4 * P], ACT.Copy).then_inc(S["xrt_copied"], 1)

            def gelu(t, n, u):
                c0 = act.value_load(tile_w[0:1, 2, bass.ds(t, 1)], min_val=0, max_val=(E - 1) * FC)
                hp = (pb, pc)[u]
                wait(act, "ghl_ready", 2 * (t - 1))
                for f in range(FC):
                    wait(act, "h_ready", FC * t + 2 * (f // 2) + 2)
                    A.activation(g[:, u, f, :], hp[:, f * TILE:(f + 1) * TILE], ACT.Gelu, scale=1.0 / WSCALE,
                                 bias=b1[:, bass.ds(c0 + f, 1)]).then_inc(S["g_ready"], 1)

            copy_turned(0, 0, 0)
            copy_turned(1, 0, 1)
            gelu(0, 0, 0)

            def step(t, n, u):
                if not isinstance(t, int) or t + 2 < TILES:
                    copy_turned(t + 2, n + 1, u)
                if not isinstance(t, int) or t + 1 < TILES:
                    gelu(t + 1, n + u, 1 - u)

            tiles(act, step)

            with act.Fori(0, PAIRS) as j:
                for u in range(2):
                    i = 2 * j + u
                    act.wait_ge(S["o_ready"], i + 1)
                    act.dma_start(out_img[bass.ds(i, 1)].rearrange("a c l -> c (a l)"), o[:, u, :]).then_inc(S[f"out_{u}"], 16)
            act.wait_ge(S["out_0"], 16 * PAIRS)
            act.wait_ge(S["out_1"], 16 * PAIRS)

        @block.vector
        def _(dve):
            V = nc.vector

            class Chain:

                def __init__(self, name, base):
                    self.name, self.base, self.n = name, base, 0

                def __call__(self, ins):
                    ins.then_inc(S[self.name], 1)
                    self.n += 1
                    dve.wait_ge(S[self.name], self.base + self.n)

            def bc_last(ap, n):
                return ap.rearrange("p (t k) -> p t k", k=1).broadcast_to([ap.shape[0], ap.shape[1], n])

            def bc_mid(ap, n):
                return ap.rearrange("p (k e) -> p k e", k=1).broadcast_to([ap.shape[0], n, ap.shape[1]])

            def newton(link, r, v, t0, t1, out_):
                link(V.scalar_tensor_tensor(out=t0, in0=r, scalar=-0.5, in1=r, op0=ALU.mult, op1=ALU.mult))
                link(V.tensor_tensor(t1, t0, v, ALU.mult))
                link(V.scalar_tensor_tensor(out=out_, in0=t1, scalar=1.5, in1=r, op0=ALU.add, op1=ALU.mult))

            dve.wait_ge(S["pool_const"], POOL_CONSTS)
            dve.wait_ge(S["w_loaded"], 16 * W_LOADS)
            link = Chain("dve_set", 0)
            chan_bn = chan[:, 2:10].rearrange("p (l k) -> p l k", l=2)
            V.tensor_scalar(bn[:, :, 0], chan_bn[:, :, 3], EPS, None, ALU.add).then_inc(S["bn_ln"], 1)
            link(V.tensor_scalar(b2_tmp[:, 0, :], b2_raw[:, :], WSCALE, None, ALU.mult))
            link(V.scalar_tensor_tensor(out=b2_tmp[:, 1, :], in0=b2_raw[:, :], scalar=WSCALE, in1=b2_tmp[:, 0, :], op0=ALU.mult, op1=ALU.subtract))
            assert link.n == SET_B2
            dve.wait_ge(S["bn_rstd"], 1)
            dve.wait_ge(S["bn_ln"], 1)
            newton(link, bn[:, :, 1], bn[:, :, 0], bn[:, :, 3], bn[:, :, 4], bn[:, :, 5])
            link(V.tensor_tensor(bn[:, :, 6], bn[:, :, 5], chan_bn[:, :, 0], ALU.mult))
            link(V.tensor_tensor(bn[:, :, 3], chan[:, 0:2], chan_bn[:, :, 2], ALU.subtract))
            link(V.tensor_tensor(bn[:, :, 4], bn[:, :, 3], bn[:, :, 6], ALU.mult))
            link(V.tensor_tensor(bn[:, :, 7], bn[:, :, 4], chan_bn[:, :, 1], ALU.add))
            dve.wait_ge(S["w_turned"], 3)
            V.tensor_copy(w_t[:, :, :].rearrange("p n c -> p (n c)"), pa[:, 0:4 * P]).then_inc(S["w_copied"], 1)
            V.tensor_copy(b1[:, :], pb[:, 0:E * FC]).then_inc(S["w_copied"], 1)
            V.tensor_tensor(wr_c[:, :], wr[:, :], pc[:, 0:E], ALU.subtract).then_inc(S["w_copied"], 1)
            for tap in range(TAPS):
                last = V.tensor_scalar(tap_diag[:, tap, :], ident[:], dw_w[:, tap:tap + 1], None, ALU.mult)
            last.then_inc(S["consts_ready"], 1)

            def s1_stats(link, n, nj, nu):
                wait(dve, f"x_loaded_{nu}", 16 * nj + 16)
                V.bn_stats(gst[:, 0:6], xb[:, nu, 0:HALF])
                link(V.bn_stats(gst[:, 6:12], xb[:, nu, HALF:L]))
                stats = gst[:, :].rearrange("p (q k) -> p k q", k=3)
                link(V.tensor_tensor(gs[:, 0:4], stats[:, 1], stats[:, 1], ALU.mult))
                V.tensor_reduce(gs[:, 8:9], stats[:, 1], AX.X, ALU.add)
                V.tensor_reduce(gs[:, 4:5], gs[:, 0:4], AX.X, ALU.add)
                link(V.tensor_reduce(gs[:, 5:6], stats[:, 2], AX.X, ALU.add))
                V.scalar_tensor_tensor(out=gs[:, 9:10], in0=gs[:, 4:5], scalar=float(L // 4), in1=gs[:, 5:6],
                                       op0=ALU.mult, op1=ALU.add).then_inc(S["gstat_ready"], 1)

            def s1_variance(link, n):
                wait(dve, "gmean_ready", n + 1)
                V.tensor_scalar(gs[:, 14:15], pa[:, 0:1], 0.25, None, ALU.mult)
                V.tensor_scalar(gs[:, 15:16], pa[:, 1:2], 1.0 / L, None, ALU.mult)
                link(V.tensor_scalar(gs[:, 16:17], pa[:, 0:1], -0.25, None, ALU.mult))
                link(V.scalar_tensor_tensor(out=gs[:, 17:18], in0=gs[:, 14:15], scalar=gs[:, 16:17], in1=gs[:, 15:16], op0=ALU.mult, op1=ALU.add))
                V.tensor_scalar(gs[:, 18:19], gs[:, 17:18], EPS, None, ALU.add).then_inc(S["gvar_ready"], 1)

            def s1_scale(link, n):
                wait(dve, "grstd_raw", n + 1)
                wait(dve, "gvar_ready", n + 1)
                newton(link, gs[:, 19:20], gs[:, 18:19], gs[:, 20:21], gs[:, 21:22], gs[:, 22:23])
                V.tensor_tensor(gs[:, 23:24], gs[:, 16:17], gs[:, 22:23], ALU.mult).then_inc(S["gnorm_ready"], 1)

            def s1_mask(link, n):
                wait(dve, "h1_ready", n + 1)
                wait(dve, "pw_ready", n)
                link(V.tensor_reduce(gs[:, 24:25], h1[:, :], AX.X, ALU.max))
                link(V.tensor_scalar(gs[:, 25:26], gs[:, 24:25], DW_THRESH, None, ALU.is_ge))
                V.tensor_scalar(pw_masked[:], w_t[:, 3, :], gs[:, 25:26], None, ALU.mult).then_inc(S["pwm_ready"], 1)

            def s1_add(link, n, nu):
                wait(dve, "h2_ready", n + 1)
                link(V.tensor_reduce(gs[:, 26:27], h2[:, :], AX.X, ALU.max))
                link(V.tensor_scalar(gs[:, 27:28], gs[:, 26:27], PW_THRESH, None, ALU.is_ge))
                V.scalar_tensor_tensor(out=x1[:, nu, :], in0=h2[:, :], scalar=gs[:, 27:28], in1=xb[:, nu, :],
                                       op0=ALU.mult, op1=ALU.add).then_inc(S["x1_ready"], 1)

            def ln_stats(link, w, pair, done):
                for t in range(NT):
                    last = V.bn_stats(st[:, w, 6 * t:6 * t + 6], pair[0:TT, t * P:(t + 1) * P])
                link(last)
                stats = st[:, w, :].rearrange("p (t k) -> p k t", k=6)
                V.tensor_tensor(ln[:, w, 0, :], stats[:, 1], stats[:, 4], ALU.add)
                V.tensor_tensor(ln[:, w, 2, :], stats[:, 2], stats[:, 5], ALU.add)
                link(V.tensor_tensor(ln[:, w, 1, :], stats[:, 1], stats[:, 4], ALU.subtract))
                link(V.tensor_tensor(ln[:, w, 3, :], ln[:, w, 1, :], ln[:, w, 1, :], ALU.mult))
                link(V.scalar_tensor_tensor(out=ln[:, w, 4, :], in0=ln[:, w, 3, :], scalar=P / 4.0, in1=ln[:, w, 2, :], op0=ALU.mult, op1=ALU.add))
                V.tensor_scalar(ln[:, w, 5, :], ln[:, w, 4, :], 1.0 / P, EPS, ALU.mult, ALU.add).then_inc(S[done], 1)

            def ln_scale(link, w, raw, var, value, done):
                wait(dve, raw, value)
                wait(dve, var, value)
                newton(link, ln[:, w, 6, :], ln[:, w, 5, :], ln[:, w, 3, :], ln[:, w, 4, :], ln[:, w, 1, :])
                V.scalar_tensor_tensor(out=ln[:, w, 2, :], in0=ln[:, w, 0, :], scalar=-0.5, in1=ln[:, w, 1, :],
                                       op0=ALU.mult, op1=ALU.mult).then_inc(S[done], 1)

            def rt3(k):
                return rt[:, k, :].rearrange("p (t e) -> p t e", e=E)

            def pick(link, values, best, out_mask):
                link(V.tensor_reduce(rs[:, best, :], rt3(values), AX.X, ALU.max))
                link(V.tensor_tensor(rt3(1), rt3(values), bc_last(rs[:, best, :], E), ALU.is_equal))
                link(V.tensor_tensor(rt3(2), rt3(1), bc_mid(descend[0:TT, :], NT), ALU.mult))
                link(V.tensor_reduce(rs[:, 3, :], rt3(2), AX.X, ALU.max))
                link(V.tensor_tensor(rt3(out_mask), rt3(2), bc_last(rs[:, 3, :], E), ALU.is_equal))

            def s2(link1, link, i, j, u, last_image):
                n, nu = i + 1, 1 - u
                nj = j + u
                if not last_image:
                    s1_stats(link1, n, nj, nu)
                wait(dve, "t1_ready", i + 1)
                ln_stats(link, 0, pb, "var1_ready")
                if not last_image:
                    s1_variance(link1, n)
                ln_scale(link, 0, "rstd1_raw", "var1_ready", i + 1, "norm1_ready")
                if not last_image:
                    s1_scale(link1, n)
                wait(dve, "xnt_ready", i + 1)
                V.tensor_copy(xt[:, :].rearrange("p (t k) -> p t k", k=TT), pc[:, 0:NT * P].rearrange("p (t k) -> p t k", k=P)[:, :, 0:TT]).then_inc(S["xt_ready"], 1)
                wait(dve, "q_ready", i + 1)
                V.tensor_scalar(sq[:, :], pd[:, 0:L], Q_THRESH, None, ALU.is_ge).then_inc(S["sq_ready"], 1)
                wait(dve, "k_ready", i + 1)
                V.tensor_scalar(sk[:, :], pb[:, 0:L], K_THRESH, None, ALU.is_ge).then_inc(S["sk_ready"], 1)
                wait(dve, "v_ready", i + 1)
                V.tensor_scalar(sv[:, :], pc[0:TT, 0:NT * P], V_THRESH, None, ALU.is_ge).then_inc(S["sv_ready"], 1)
                if not last_image:
                    s1_mask(link1, n)
                wait(dve, "seen_ready", NT * i + NT)
                diag = seen.rearrange("p (t k) -> p t k", k=L + TT)[:, :, 0:TT]
                V.tensor_tensor(diag, diag, bc_mid(causal[0:TT, :], NT), ALU.mult).then_inc(S["tri_ready"], 1)
                wait(dve, f"t2_kept_{u}", 16 * j)
                wait(dve, "att_ready", i + 1)
                wait(dve, "x1_ready", i + 1)
                V.tensor_tensor(t2[:, u, :].rearrange("p (h c) -> p h c", h=2), pc[:, :].rearrange("p (h c) -> p h c", h=2)[:, :, 0:HALF],
                                x1[:, u, :].rearrange("p (h c) -> p h c", h=2), ALU.add).then_inc(S["t2_ready"], 1)
                if not last_image:
                    s1_add(link1, n, nu)
                wait(dve, "t2t_ready", i + 1)
                ln_stats(link, 1, pd, "var2_ready")
                ln_scale(link, 1, "rstd2_raw", "var2_ready", i + 1, "norm2_ready")
                wait(dve, "norm2_ready", i + 1)
                wait(dve, "logit_ready", i + 1)
                V.tensor_tensor(rt3(0), pb[0:TT, 0:NT * E].rearrange("p (t e) -> p t e", e=E), bc_last(ln[:, 1, 1, :], E), ALU.mult).then_inc(S["logit_read"], 1)
                wait(dve, "logit_read", i + 1)
                pick(link, 0, 0, 4)
                link(V.scalar_tensor_tensor(out=rt[:, 5, :], in0=rt[:, 4, :], scalar=-3.0e38, in1=rt[:, 0, :], op0=ALU.mult, op1=ALU.add))
                pick(link, 5, 2, 6)
                V.tensor_tensor(rs[:, 4, :], rs[:, 2, :], rs[:, 0, :], ALU.subtract).then_inc(S["gap_ready"], 1)
                V.tensor_tensor(chosen[:, 0:NT * E], rt[:, 4, :], rt[:, 6, :], ALU.add).then_inc(S["chosen_ready"], 1)
                wait(dve, f"sent_{u}", 16 * 2 * NT * j)
                fields = rows[:, u, :, 2 * P:ROW].bitcast(F32)
                V.tensor_scalar(fields[:, :, 0], token[:, :], 2.0, None, ALU.mult)
                V.tensor_scalar(fields[:, :, 1], rs[:, 3, :], -1.0, float(E), ALU.mult, ALU.add)
                wait(dve, "gexp_ready", i + 1)
                link(V.tensor_scalar(rs[:, 6, :], rs[:, 5, :], 1.0, None, ALU.add))
                link(V.reciprocal(rs[:, 7, :], rs[:, 6, :]))
                link(V.tensor_tensor(rs[:, 8, :], rs[:, 5, :], rs[:, 7, :], ALU.mult))
                link(V.tensor_tensor(rs[:, 9, :], rs[:, 8, :], rs[:, 7, :], ALU.subtract))
                V.tensor_scalar(fields[:, :, 2], rs[:, 7, :], 1.0 / WSCALE, None, ALU.mult)
                V.tensor_scalar(fields[:, :, 3], rs[:, 9, :], 1.0 / WSCALE, None, ALU.mult)
                link(V.tensor_scalar(token[:, :], token[:, :], float(L), None, ALU.add))
                wait(dve, "hi_ready", i + 1)
                V.tensor_tensor(rows[:, u, :, P:2 * P], xf[:, :, :], rows[:, u, :, 0:P], ALU.subtract)
                wait(dve, "rank_ready", i + 1)
                link(V.tensor_tensor(rt3(7), pc[0:TT, 0:NT * E].rearrange("p (t e) -> p t e", e=E), bc_mid(base[0:TT, :], NT), ALU.add))
                V.tensor_tensor(base[:, :], base[:, :], pc[:, NT * E:(NT + 1) * E], ALU.add).then_inc(S["rank_read"], 1)
                wait(dve, "rank_read", i + 1)
                V.tensor_tensor(rt3(8), rt3(4), rt3(7), ALU.mult)
                link(V.tensor_tensor(rt3(9), rt3(6), rt3(7), ALU.mult))
                V.tensor_reduce(rs[:, 10, :], rt3(8), AX.X, ALU.add)
                link(V.tensor_reduce(rs[:, 11, :], rt3(9), AX.X, ALU.add))
                V.tensor_copy(pos[:, u, :, :].rearrange("p t k -> p k t"), rs[:, 10:12, :]).then_inc(S["rows_ready"], 1)
                if u == 0:
                    wait(dve, "w_hi_ready", 2 * j + 2)
                    for w, stage in ((w1, 0), (w2, 1)):
                        V.scalar_tensor_tensor(out=w[:, 1, bass.ds(j * HID, HID)], in0=w_stage[:, stage, :], scalar=WSCALE,
                                               in1=w[:, 0, bass.ds(j * HID, HID)], op0=ALU.mult, op1=ALU.subtract).then_inc(S["w_lo_ready"], 1)

            def body(i, j, u, last_image):
                link1, link2 = Chain("dve_s1", DVE_S1 * (i + 1)), Chain("dve_s2", DVE_S2 * i)
                s2(link1, link2, i, j, u, last_image)
                assert link1.n in (0, DVE_S1) and link2.n == DVE_S2, (link1.n, link2.n)

            first = Chain("dve_s1", 0)
            s1_stats(first, 0, 0, 0)
            s1_variance(first, 0)
            s1_scale(first, 0)
            s1_mask(first, 0)
            s1_add(first, 0, 0)
            assert first.n == DVE_S1, first.n
            images(dve, body)

            link = Chain("dve_tab", 0)
            link(V.scalar_tensor_tensor(out=tsmall[:, 0, :], in0=descend[:, :], scalar=float(REGION), in1=base[:, :], op0=ALU.mult, op1=ALU.add))
            link(V.tensor_scalar(tsmall[:, 1, :], tsmall[:, 0, :], -float(E * REGION), None, ALU.add))
            link(V.tensor_tensor(tcount[:, :, :], bc_last(tsmall[:, 1, :], MAXT), tcount[:, :, :], ALU.is_gt))
            link(V.tensor_reduce(tsmall[:, 2, :], tcount[:, :, :], AX.X, ALU.add))
            V.tensor_scalar(tsmall[:, 3, :], tsmall[:, 2, :], -float(TILE), float(REGION), ALU.mult, ALU.add)
            link(V.tensor_copy(tsmall[:, 4, 0:1], tsmall[:, 2, 0:1]))
            for e in range(1, E):
                link(V.tensor_tensor(tsmall[:, 4, e:e + 1], tsmall[:, 4, e - 1:e], tsmall[:, 2, e:e + 1], ALU.add))
            ended = tbig[:, 0, :].rearrange("p (t e) -> p t e", e=E)
            skipped = tbig[:, 1, :].rearrange("p (t e) -> p t e", e=E)
            link(V.tensor_tensor(ended, bc_last(tile_no[:, :], E), bc_mid(tsmall[:, 4, :], TILES), ALU.is_ge))
            V.tensor_reduce(tile_expert[:, :], ended, AX.X, ALU.add)
            link(V.tensor_tensor(skipped, ended, bc_mid(tsmall[:, 3, :], TILES), ALU.mult))
            link(V.tensor_reduce(tcol[:, 0, :], skipped, AX.X, ALU.add))
            V.scalar_tensor_tensor(out=tile_row[:, :], in0=tile_no[:, :], scalar=float(TILE), in1=tcol[:, 0, :], op0=ALU.mult, op1=ALU.add)
            for n, width in enumerate((HID, P, FC)):
                V.tensor_scalar(tile_w[:, n, :], tile_expert[:, :], float(E - 1), float(width), ALU.min, ALU.mult)
            V.tensor_copy(pad_at[:, :], base[:, :]).then_inc(S["tables_ready"], 1)

            def fields(t, n, u):
                f = xr[:, u, :, 2 * P:ROW].bitcast(F32)
                wait(dve, f"stored_{u}", 32 * n)
                wait(dve, f"xr_loaded_{u}", 16 * n + 16)
                link = Chain("dve_b", 2 * t)
                link(V.tensor_scalar(small[:, u, 0, :], f[:, :, 1], tile_expert[:, bass.ds(t, 1)], None, ALU.is_equal))
                link(V.tensor_tensor(small[:, u, 1, :], small[:, u, 0, :], f[:, :, 3], ALU.mult))
                V.tensor_tensor(small[:, u, 2, :], small[:, u, 1, :], f[:, :, 2], ALU.add)
                V.tensor_tensor(dest[:, u, :], small[:, u, 0, :], f[:, :, 0], ALU.add).then_inc(S["dest_ready"], 1)

            def split(t, n, u, h):
                c = slice(2 * h * TILE, 2 * (h + 1) * TILE)
                gv = g[:, u, 2 * h:2 * h + 2, :].rearrange("p f k -> p (f k)")
                wait(dve, "y_ready", t - 1)
                wait(dve, "g_ready", FC * t + 2 * h + 2)
                V.tensor_copy(ghl[:, u, 0, c], gv).then_inc(S["g_hi_ready"], 1)
                wait(dve, "g_hi_ready", 2 * t + h + 1)
                V.tensor_tensor(ghl[:, u, 1, c], gv, ghl[:, u, 0, c], ALU.subtract).then_inc(S["ghl_ready"], 1)

            def gated(t, n, u):
                wait(dve, "y_ready", t + 1)
                wait(dve, "dest_ready", t + 1)
                for s in range(2):
                    last = V.tensor_scalar(y[:, u, s, :], pd[:, u * BANK + s * P:u * BANK + (s + 1) * P], small[:, u, 2, s:s + 1], None, ALU.mult)
                last.then_inc(S["y_copied"], 1)

            fields(0, 0, 0)
            split(0, 0, 0, 0)
            split(0, 0, 0, 1)

            def step(t, n, u):
                more = not isinstance(t, int) or t + 1 < TILES
                if more:
                    fields(t + 1, n + u, 1 - u)
                gated(t, n, u)
                if more:
                    split(t + 1, n + u, 1 - u, 0)
                    split(t + 1, n + u, 1 - u, 1)

            tiles(dve, step)

            def sum_rows(i, j, u):
                wait(dve, "yt_ready", i - 1)
                wait(dve, f"yl_loaded_{u}", 16 * j + 16)
                V.tensor_tensor(ysum[:, u, :, :], yl[:, u, :, 0, :], yl[:, u, :, 1, :], ALU.add).then_inc(S["ysum_ready"], 1)

            def add_rows(i, j, u):
                wait(dve, "yt_ready", i + 1)
                wait(dve, f"out_{u}", 16 * j)
                V.tensor_tensor(o[:, u, :].rearrange("p (t k) -> p t k", k=TT), (pa, pb)[u][:, 0:NT * P].rearrange("p (t k) -> p t k", k=P)[:, :, 0:TT],
                                t2_all[:, bass.ds(i * L, L)].rearrange("p (t k) -> p t k", k=TT), ALU.add).then_inc(S["o_ready"], 1)

            dve.wait_ge(S["t2_kept_0"], 16 * PAIRS)
            dve.wait_ge(S["t2_kept_1"], 16 * PAIRS)
            sum_rows(0, 0, 0)
            sum_rows(1, 0, 1)
            add_rows(0, 0, 0)
            add_rows(1, 0, 1)
            with dve.Fori(1, PAIRS) as j:
                sum_rows(2 * j, j, 0)
                sum_rows(2 * j + 1, j, 1)
                add_rows(2 * j, j, 0)
                add_rows(2 * j + 1, j, 1)


_INS = ["x"] + ["L0_conv_" + n for n in ("dw_w", "dw_b", "bn1_g", "bn1_b", "bn1_m", "bn1_v", "pw_w", "pw_b", "bn2_g", "bn2_b", "bn2_m", "bn2_v")] \
    + ["L1_attn_" + n for n in ("Wq", "Wk", "Wv")] + ["L1_ffn_" + n for n in ("Wr", "W1", "b1", "W2", "b2")]


def kernel(**inputs):
    import numpy as _np
    import concourse.bacc as _bacc
    from concourse import mybir as _mybir
    from concourse.bass_utils import run_bass_kernel_spmd as _run

    nc = _bacc.Bacc("TRN2", target_bir_lowering=False, num_devices=1)
    arrays, args = {}, {}
    for name in _INS:
        v = _np.ascontiguousarray(inputs[name])
        arrays[f"in_{name}"] = v
        args[name] = nc.dram_tensor(f"in_{name}", v.shape, _mybir.dt.from_np(v.dtype), kind="ExternalInput").ap()
    shape = tuple(inputs["x"].shape)
    out = nc.dram_tensor("out_0", shape, _mybir.dt.float32, kind="ExternalOutput").ap()
    build(nc, args, out)
    r = _run(nc, [arrays], core_ids=[0])
    return r.results[0]["out_0"]
```

```python
from contextlib import ExitStack

import concourse.bass as bass
from concourse import mybir

F32 = mybir.dt.float32
F16 = mybir.dt.float16
BF16 = mybir.dt.bfloat16
I32 = mybir.dt.int32
U32 = mybir.dt.uint32
ALU = mybir.AluOpType
ACT = mybir.ActivationFunctionType
AX = mybir.AxisListType

P = 128
IMAGES, SIDE = 16, 28
L = SIDE * SIDE
HALF = L // 2
TOKENS = IMAGES * L
TT, NT = 112, 7
PAD = SIDE + 2
TAPS = 9
EPS = 1e-5
GROUP = 4
DW_THRESH, PW_THRESH = 4.0, 0.001
Q_THRESH, K_THRESH, V_THRESH = 0.25, 0.25, 0.3
E, HID = 8, 512
FC = HID // P
WSCALE = 64.0
TILE = 256
REGION = TOKENS + TILE
TILES = (2 * TOKENS + E * (TILE - 1)) // TILE
LEAST_TILES = 2 * TOKENS // TILE
XROWS = E * REGION + (TILES - LEAST_TILES + 1) * TILE
ROW = 2 * P + 6
SKIP = 1.0e6
MAXT = TOKENS // TILE + 1
BANK = 512
DEEP = 4
LOOP_END = (TILES - 3) // DEEP
POOL_CONSTS = 23
W_LOADS = 18
SET_B2 = 2
DVE_S1, DVE_S2 = 14, 33


def build(nc, a, out):
    xs = nc.dram_tensor("dispatched_rows", (XROWS, ROW // 2), U32, kind="Internal").ap()
    ys = nc.dram_tensor("expert_rows", (2 * TOKENS, P), F32, kind="Internal").ap()
    x_img = a["x"].rearrange("b c h w -> b c (h w)")
    out_img = out.rearrange("b c h w -> b c (h w)")

    with ExitStack() as ctx:
        def sb(name, shape, dt):
            return ctx.enter_context(nc.sbuf_tensor(name, shape, dt))

        def sem(name):
            return ctx.enter_context(nc.semaphore(name))

        psum = [ctx.enter_context(nc.psum_tensor(f"pair_{n}", [P, 2 * BANK], F32)) for n in "abcd"]
        pa, pb, pc, pd = psum

        ident = sb("ident", [P, P], F32)
        ident16 = sb("ident16", [P, P], F16)
        group_avg = sb("group_avg", [P, P], F32)
        before = sb("before", [P, P], BF16)
        ones = sb("ones", [P, P], BF16)
        causal = sb("causal", [P, TT], BF16)
        w_raw = sb("w_raw", [P, 4, P], F32)
        w_t = sb("w_t", [P, 4, P], F32)
        chan = sb("chan", [P, 10], F32)
        dw_w = sb("dw_w", [P, TAPS], F32)
        tap_diag = sb("tap_diag", [P, TAPS, P], F32)
        bn = sb("bn", [P, 2, 8], F32)
        wr = sb("wr", [P, E], F32)
        wr_c = sb("wr_c", [P, E], F32)
        avg_all = sb("avg_all", [P, P], F32)
        w1 = sb("w1", [P, 2, E * HID], F16)
        w2 = sb("w2", [P, 2, E * HID], F16)
        w_stage = sb("w_stage", [P, 2, HID], F32)
        b1_raw = sb("b1_raw", [E * FC, P], F32)
        b1 = sb("b1", [P, E * FC], F32)
        b2_raw = sb("b2_raw", [1, E * P], F32)
        b2 = sb("b2", [P, E * P], F16)
        b2_tmp = sb("b2_tmp", [1, 2, E * P], F16)
        two_rows = sb("two_rows", [P, P], F16)

        xb_x1 = sb("xb_x1", [P, 4 * L], F32)
        xb = xb_x1[:, 0:2 * L].rearrange("p (u l) -> p u l", u=2)
        x1 = xb_x1[:, 2 * L:4 * L].rearrange("p (u l) -> p u l", u=2)
        padx = sb("padx", [P, 2, PAD, PAD], F32)
        h1 = sb("h1", [P, L], F32)
        h2 = sb("h2", [P, L], F32)
        gs = sb("gs", [P, 32], F32)
        gst = sb("gst", [P, 12], F32)
        pw_masked = sb("pw_masked", [P, P], F32)
        st = sb("st", [TT, 2, NT * 6], F32)
        ln = sb("ln", [TT, 2, 8, NT], F32)
        xn = sb("xn", [TT, NT, P], F32)
        xt = sb("xt", [P, L], F32)
        xf = sb("xf", [TT, NT, P], F32)
        sq = sb("sq", [P, L], BF16)
        sk = sb("sk", [P, L], BF16)
        sv = sb("sv", [TT, NT * P], BF16)
        seen_g = sb("seen_g", [P, NT * (L + TT)], BF16)
        seen = seen_g[0:TT, :]
        t2 = sb("t2", [P, 2, L], F32)
        t2_all = sb("t2_all", [P, IMAGES * L], F32)
        rows = sb("rows", [TT, 2, NT, ROW], F16)
        pos = sb("pos", [TT, 2, NT, 2], I32)
        rt = sb("rt", [TT, 12, NT * E], F32)
        rs = sb("rs", [TT, 12, NT], F32)
        chosen = sb("chosen", [TT, (NT + 1) * E], BF16)
        base = sb("base", [P, E], F32)
        descend = sb("descend", [P, E], F32)
        token = sb("token", [TT, NT], F32)

        tcount = sb("tcount", [P, E, MAXT], F32)
        tsmall = sb("tsmall", [P, 8, E], F32)
        tbig = sb("tbig", [P, 2, TILES * E], F32)
        tcol = sb("tcol", [P, 4, TILES], F32)
        tile_no = sb("tile_no", [P, TILES], F32)
        tile_row = sb("tile_row", [P, TILES], I32)
        tile_expert = sb("tile_expert", [P, TILES], F32)
        tile_w = sb("tile_w", [P, TILES], I32)
        pad_at = sb("pad_at", [P, E], I32)
        pad_rows = sb("pad_rows", [P, 2, ROW], F16)

        xr = sb("xr", [P, DEEP, 2, ROW], F16)
        xrt = sb("xrt", [P, 2, 4, P], F16)
        g = seen_g[:, 0:4 * FC * TILE].bitcast(F32).rearrange("p (u f k) -> p u f k", u=2, f=FC)
        ghl = xb_x1[:, 0:2 * FC * TILE].bitcast(F16).rearrange("p (u h k) -> p u h k", u=2, h=2)
        y = xb_x1[:, 2 * FC * TILE:2 * FC * TILE + DEEP * 2 * P].rearrange("p (u s c) -> p u s c", u=DEEP, s=2)
        small = sb("small", [P, DEEP, 4, 2], F32)
        dest = sb("dest", [P, DEEP, 2], I32)

        w1_place = w1[:, :, :].rearrange("p n c -> p (n c)").bitcast(F32)
        w2_place = w2[:, :, :].rearrange("p n c -> p (n c)").bitcast(F32)
        yl = w1_place[0:TT, 0:4 * NT * P].rearrange("p (u t k d) -> p u t k d", u=2, t=NT, k=2)
        ysum = w2_place[0:TT, 0:2 * NT * P].rearrange("p (u t d) -> p u t d", u=2, t=NT)
        o = w2_place[:, 2 * NT * P:2 * NT * P + 2 * L].rearrange("p (u l) -> p u l", u=2)

        S = {n: sem(n) for n in (
            "w_loaded", "pool_const", "w_turned", "w_copied", "consts_ready", "bn_ln", "bn_rstd",
            "x_loaded_0", "x_loaded_1", "gstat_ready", "gmean_ready", "gvar_ready", "grstd_raw",
            "gnorm_ready", "xn_ready", "conv_ready", "h1_ready", "pwm_ready", "pw_ready",
            "h2_ready", "x1_ready", "dve_s1", "dve_s2", "act_chain",
            "t1_ready", "var1_ready", "rstd1_raw", "norm1_ready", "xn1_ready", "xnt_ready",
            "xt_ready", "q_ready", "k_ready", "v_ready", "sq_ready", "sk_ready", "sv_ready",
            "score_ready", "seen_ready", "tri_ready", "att_ready", "t2_ready", "t2_kept_0",
            "t2_kept_1", "t2t_ready", "logit_ready", "logit_read", "var2_ready", "rstd2_raw", "norm2_ready",
            "xn2_ready", "hi_ready", "gap_ready", "gexp_ready", "chosen_ready", "rank_ready", "rank_read",
            "rows_ready", "sent_0", "sent_1", "stage_loaded", "w_hi_ready", "w_lo_ready",
            "tables_ready", "pad_ready", "padded", "dve_tab", "dve_b",
            "xr_loaded_0", "xr_loaded_1", "xr_loaded_2", "xr_loaded_3", "arg_ready", "tanh_ready", "gate_ready", "xrt_ready", "xrt_copied", "h_ready", "g_ready",
            "g_hi_ready", "ghl_ready", "y_ready", "y_copied", "dest_ready", "stored_0", "stored_1", "stored_2", "stored_3",
            "yl_loaded_0", "yl_loaded_1", "ysum_ready", "yt_ready", "o_ready", "out_0", "out_1",
            "b2_moved", "dve_set", "gates",
        )}

        block = ctx.enter_context(nc.Block())
        PAIRS = IMAGES // 2

        def wait(eng, name, value):
            if not (isinstance(value, int) and value <= 0):
                eng.wait_ge(S[name], value)

        def images(eng, body):
            body(0, 0, 0, False)
            body(1, 0, 1, False)
            with eng.Fori(1, PAIRS - 1) as j:
                body(2 * j, j, 0, False)
                body(2 * j + 1, j, 1, False)
            body(IMAGES - 2, PAIRS - 1, 0, False)
            body(IMAGES - 1, PAIRS - 1, 1, True)

        def tiles(eng, group):
            group(0, 0, DEEP)
            with eng.Fori(1, LOOP_END) as n:
                group(DEEP * n, n, DEEP)
            for t in range(DEEP * LOOP_END, TILES, DEEP):
                group(t, t // DEEP, min(DEEP, TILES - t))

        def table(engine, entries, t, count, most):
            if isinstance(t, int):
                count = min(count, TILES - t)
            return nc.values_load_multi_w_load_instructions(
                entries[0:1, bass.ds(t, count)], engines=[engine], min_val=0, max_val=most,
                skip_runtime_bounds_check_because="VectorE has bounded every entry of the tables")[1]

        def later(t, n, u, d):
            if isinstance(t, int) and t + d >= TILES:
                return None
            return t + d, n + (u + d) // DEEP, (u + d) % DEEP

        @block.sync
        def _(sp):
            with nc.allow_non_contiguous_dma(reason="small parameters"):
                for n, name in enumerate(("L1_attn_Wq", "L1_attn_Wk", "L1_attn_Wv")):
                    sp.dma_start(w_raw[:, n, :], a[name]).then_inc(S["w_loaded"], 16)
                sp.dma_start(w_raw[:, 3, :], a["L0_conv_pw_w"].rearrange("o c h w -> o (c h w)")).then_inc(S["w_loaded"], 16)
                sp.dma_start(dw_w[:, :], a["L0_conv_dw_w"].rearrange("c k h w -> c (k h w)")).then_inc(S["w_loaded"], 16)
                for n, name in enumerate(("dw_b", "pw_b", "bn1_g", "bn1_b", "bn1_m", "bn1_v", "bn2_g", "bn2_b", "bn2_m", "bn2_v")):
                    sp.dma_start(chan[:, n:n + 1], a["L0_conv_" + name].rearrange("(c k) -> c k", k=1)).then_inc(S["w_loaded"], 16)
                sp.dma_start(wr[:, :], a["L1_ffn_Wr"]).then_inc(S["w_loaded"], 16)
                sp.dma_start(b1_raw[:, :], a["L1_ffn_b1"].rearrange("e (f p) -> (e f) p", p=P)).then_inc(S["w_loaded"], 16)
                sp.dma_start(b2_raw[:, :], a["L1_ffn_b2"].rearrange("(k e) d -> k (e d)", k=1)).then_inc(S["w_loaded"], 16)
            sp.dma_start(xb[:, 0, :], x_img[0]).then_inc(S["x_loaded_0"], 16)
            sp.dma_start(xb[:, 1, :], x_img[1]).then_inc(S["x_loaded_1"], 16)
            wait(sp, "pad_ready", 3)
            spare = TILES - LEAST_TILES + 1
            for n in range(spare):
                r0 = E * REGION + n * TILE
                sp.dma_start(xs[r0:r0 + TILE, :].rearrange("(s p) c -> p s c", p=P), pad_rows[:, :, :].bitcast(U32)).then_inc(S["padded"], 16)
            wait(sp, "dve_set", SET_B2)
            sp.dma_start(b2[0:1, :], b2_tmp[:, 0, :]).then_inc(S["b2_moved"], 16)
            sp.dma_start(b2[1:2, :], b2_tmp[:, 1, :]).then_inc(S["b2_moved"], 16)

            def body(i, j, u, last):
                if u == 0:
                    wait(sp, "w_lo_ready", 2 * j)
                    sp.dma_start(w_stage[:, 0, :], a["L1_ffn_W1"][bass.ds(j, 1)].rearrange("a d h -> d (a h)")).then_inc(S["stage_loaded"], 16)
                    sp.dma_start(w_stage[:, 1, :].rearrange("p (f d) -> p f d", f=FC),
                                 a["L1_ffn_W2"][bass.ds(j, 1)].rearrange("a (f p) d -> p (a f) d", p=P)).then_inc(S["stage_loaded"], 16)
                if not isinstance(i, int) or i + 2 < IMAGES:
                    wait(sp, "x1_ready", i + 1)
                    sp.dma_start(xb[:, u, :], x_img[bass.ds(i + 2, 1)].rearrange("a c l -> c (a l)")).then_inc(S[f"x_loaded_{u}"], 16)
                wait(sp, "t2_ready", i + 1)
                sp.dma_start(t2_all[:, bass.ds(i * L, L)], t2[:, u, :]).then_inc(S[f"t2_kept_{u}"], 16)

            images(sp, body)

            wait(sp, "sent_0", 16 * 2 * NT * PAIRS)
            wait(sp, "sent_1", 16 * 2 * NT * PAIRS)
            wait(sp, "tables_ready", 1)
            for e in range(E):
                at = sp.value_load(pad_at[0:1, e:e + 1], min_val=0, max_val=XROWS - TILE)
                sp.dma_start(xs[bass.ds(at, TILE), :].rearrange("(s p) c -> p s c", p=P), pad_rows[:, :, :].bitcast(U32)).then_inc(S["padded"], 16)
            wait(sp, "padded", 16 * (E + spare))

            def load_tiles(t0, n, count):
                rows_at = table(mybir.EngineType.SP, tile_row, t0, count, XROWS - TILE)
                for u in range(count):
                    t = t0 + u
                    wait(sp, "xrt_ready", t - 3)
                    wait(sp, "dest_ready", t - 3)
                    sp.wait_ge(S["tables_ready"], 1)
                    sp.dma_start(xr[:, u, :, :].bitcast(U32), xs[bass.ds(rows_at[u], TILE), :].rearrange("(s p) c -> p s c", p=P)).then_inc(S[f"xr_loaded_{u}"], 16)

            tiles(sp, load_tiles)

            for u in range(DEEP):
                wait(sp, f"stored_{u}", 32 * ((TILES - u + DEEP - 1) // DEEP))
            y_img = ys.rearrange("(b t p k) d -> b p t (k d)", b=IMAGES, t=NT, k=2)

            def load_y(i, j, u):
                wait(sp, "ysum_ready", i - 1)
                sp.dma_start(yl[:, u, :, :, :].rearrange("p t k d -> p t (k d)"),
                             y_img[bass.ds(i, 1)].rearrange("a p t d -> p (a t) d")).then_inc(S[f"yl_loaded_{u}"], 16)

            load_y(0, 0, 0)
            load_y(1, 0, 1)
            with sp.Fori(1, PAIRS) as j:
                load_y(2 * j, j, 0)
                load_y(2 * j + 1, j, 1)

        @block.gpsimd
        def _(pool):
            G = nc.gpsimd
            done = [0]

            def const(ins):
                done[0] += 1
                ins.then_inc(S["pool_const"], 1)

            def settle():
                pool.wait_ge(S["pool_const"], done[0])

            const(G.memset(ident[:], 0.0))
            const(G.memset(ident16[:], 0.0))
            const(G.memset(group_avg[:], 1.0 / GROUP))
            const(G.memset(before[:], 1.0))
            const(G.memset(causal[:], 1.0))
            const(G.memset(ones[:], 1.0))
            const(G.memset(avg_all[:], 1.0 / P))
            const(G.memset(padx[:], 0.0))
            const(G.memset(two_rows[:], 1.0))
            const(G.memset(b2[:], 0.0))
            const(G.memset(chosen[:], 0.0))
            const(G.iota(base[:], [[REGION, E]], base=0, channel_multiplier=0, allow_small_or_imprecise_dtypes=True))
            const(G.iota(descend[:], [[-1, E]], base=E, channel_multiplier=0, allow_small_or_imprecise_dtypes=True))
            const(G.iota(token[:], [[TT, NT]], base=0, channel_multiplier=1, allow_small_or_imprecise_dtypes=True))
            settle()
            const(G.affine_select(out=ident[:], in_=ident[:], compare_op=ALU.not_equal, fill=1.0, base=0, pattern=[[-1, P]], channel_multiplier=1))
            const(G.affine_select(out=ident16[:], in_=ident16[:], compare_op=ALU.not_equal, fill=1.0, base=0, pattern=[[-1, P]], channel_multiplier=1))
            ga = group_avg[:].rearrange("p (g r) -> p g r", r=GROUP)
            const(G.affine_select(out=ga, in_=ga, compare_op=ALU.is_ge, fill=0.0, base=0, pattern=[[-GROUP, P // GROUP], [0, GROUP]], channel_multiplier=1))
            const(G.affine_select(out=before[:], in_=before[:], compare_op=ALU.is_gt, fill=0.0, base=0, pattern=[[1, P]], channel_multiplier=-1))
            const(G.affine_select(out=causal[:], in_=causal[:], compare_op=ALU.is_ge, fill=0.0, base=0, pattern=[[1, TT]], channel_multiplier=-1))
            const(G.affine_select(out=two_rows[:], in_=two_rows[:], compare_op=ALU.is_ge, fill=0.0, base=1, pattern=[[0, P]], channel_multiplier=-1))
            settle()
            const(G.affine_select(out=ga, in_=ga, compare_op=ALU.is_ge, fill=0.0, base=GROUP - 1, pattern=[[GROUP, P // GROUP], [0, GROUP]], channel_multiplier=-1))
            const(G.iota(tile_no[:], [[1, TILES]], base=0, channel_multiplier=0, allow_small_or_imprecise_dtypes=True))
            const(G.iota(tcount[:], [[0, E], [TILE, MAXT]], base=0, channel_multiplier=0, allow_small_or_imprecise_dtypes=True))
            settle()
            assert done[0] == POOL_CONSTS, done
            G.memset(pad_rows[:], 0.0).then_inc(S["pad_ready"], 1)
            wait(pool, "pad_ready", 1)
            G.memset(pad_rows[:, :, 2 * P:2 * P + 2].bitcast(F32), SKIP).then_inc(S["pad_ready"], 1)
            wait(pool, "pad_ready", 2)
            G.memset(pad_rows[:, :, 2 * P + 2:ROW].bitcast(F32), 0.0).then_inc(S["pad_ready"], 1)
            def gate(name, value):
                pool.wait_ge(S[name], value)
                pool.sem_inc(S["gates"], 1)

            rows_end = pool.to_reg(XROWS - 1)
            table_end = pool.to_reg(2 * TOKENS - 1)

            def body(i, j, u, last):
                gate("rows_ready", i + 1)
                for t in range(NT):
                    for k in range(2):
                        pool.indirect_dma_start(
                            xs, bass.IndirectOffsetOnAxis(ap=pos[:, u, t, k:k + 1].bitcast(U32), axis=0),
                            rows[:, u, t, :].bitcast(U32), None, bounds_check=rows_end, oob_is_err=False).then_inc(S[f"sent_{u}"], 16)

            images(pool, body)

            def store_tiles(t0, n, count):
                for u in range(count):
                    gate("y_copied", t0 + u + 1)
                    for s in range(2):
                        pool.indirect_dma_start(
                            ys, bass.IndirectOffsetOnAxis(ap=dest[:, u, s:s + 1].bitcast(U32), axis=0),
                            y[:, u, s, :], None, bounds_check=table_end, oob_is_err=False).then_inc(S[f"stored_{u}"], 16)

            tiles(pool, store_tiles)

        @block.tensor
        def _(pe):
            T = nc.tensor
            pe.wait_ge(S["pool_const"], POOL_CONSTS)
            pe.wait_ge(S["w_loaded"], 16 * W_LOADS)
            for n in range(4):
                last = T.transpose(pa[:, n * P:(n + 1) * P], w_raw[:, n, :], ident[:])
            last.then_inc(S["w_turned"], 1)
            T.transpose(pb[:, 0:E * FC], b1_raw[:, :], ident[0:E * FC, 0:E * FC]).then_inc(S["w_turned"], 1)
            T.matmul(pc[:, 0:E], avg_all[:], wr[:], start=True, stop=True).then_inc(S["w_turned"], 1)
            pe.wait_ge(S["w_copied"], 3)

            def group_stats(n, nj, nu):
                wait(pe, "h2_ready", n)
                wait(pe, "gstat_ready", n + 1)
                T.matmul(pa[:, 0:2], group_avg[:], gs[:, 8:10], start=True, stop=True).then_inc(S["gmean_ready"], 1)

            def conv(n, nj, nu):
                wait(pe, "xn_ready", n + 1)
                for tap in range(TAPS):
                    ky, kx = tap // 3, tap % 3
                    for h in range(2):
                        last = T.matmul(pa[:, h * BANK:h * BANK + HALF], tap_diag[:, tap, :],
                                        padx[:, nu, ky + 14 * h:ky + 14 * h + 14, kx:kx + SIDE],
                                        start=(tap == 0), stop=(tap == TAPS - 1))
                last.then_inc(S["conv_ready"], 1)

            def pointwise(n):
                wait(pe, "pwm_ready", n + 1)
                wait(pe, "h1_ready", n + 1)
                for h in range(2):
                    last = T.matmul(pa[:, h * BANK:h * BANK + HALF], pw_masked[:], h1[:, h * HALF:(h + 1) * HALF], start=True, stop=True)
                last.then_inc(S["pw_ready"], 1)

            pe.wait_ge(S["consts_ready"], 1)
            group_stats(0, 0, 0)
            conv(0, 0, 0)
            pointwise(0)

            def body(i, j, u, last_image):
                n, nu = i + 1, 1 - u
                if not last_image:
                    group_stats(n, 0, nu)
                wait(pe, "logit_read", i)
                wait(pe, "x1_ready", i + 1)
                for t in range(NT):
                    last = T.transpose(pb[0:TT, t * P:(t + 1) * P], x1[:, u, t * TT:(t + 1) * TT], ident[:])
                last.then_inc(S["t1_ready"], 1)
                if not last_image:
                    conv(n, 0, nu)
                wait(pe, "rank_read", i)
                wait(pe, "xn1_ready", i + 1)
                for t in range(NT):
                    last = T.transpose(pc[:, t * P:t * P + TT], xn[:, t, :], ident[0:TT, 0:TT])
                last.then_inc(S["xnt_ready"], 1)
                wait(pe, "xt_ready", i + 1)
                wait(pe, "xn2_ready", i)
                for pair, w, name in ((pd, 0, "q_ready"), (pb, 1, "k_ready")):
                    for c0, c1 in ((0, BANK), (BANK, L)):
                        last = T.matmul(pair[:, c0:c1], w_t[:, w, :], xt[:, c0:c1], start=True, stop=True)
                    last.then_inc(S[name], 1)
                for t in range(NT):
                    last = T.matmul(pc[0:TT, t * P:(t + 1) * P], xt[:, t * TT:(t + 1) * TT], w_t[:, 2, :], start=True, stop=True)
                last.then_inc(S["v_ready"], 1)
                for t in range(NT):
                    width = L - t * TT
                    if t == 0:
                        wait(pe, "sk_ready", i + 1)
                    if t >= 2:
                        wait(pe, "seen_ready", i * NT + t - 1)
                    pair = (pd, pb)[t % 2]
                    for c0 in range(0, width, BANK):
                        c1 = min(c0 + BANK, width)
                        last = T.matmul(pair[0:TT, c0:c1], sk[:, t * TT:(t + 1) * TT], sq[:, t * TT + c0:t * TT + c1], start=True, stop=True)
                    last.then_inc(S["score_ready"], 1)
                if not last_image:
                    pointwise(n)
                wait(pe, "tri_ready", i + 1)
                wait(pe, "sv_ready", i + 1)
                for h in range(2):
                    tiles = [t for t in range(NT) if t * TT < (h + 1) * HALF]
                    for t in tiles:
                        l0 = max(t * TT, h * HALF)
                        last = T.matmul(pc[:, h * BANK + l0 - h * HALF:h * BANK + HALF], sv[:, t * P:(t + 1) * P],
                                        seen[:, t * L + l0:t * L + (h + 1) * HALF], start=(t == 0), stop=(t == tiles[-1]))
                last.then_inc(S["att_ready"], 1)
                wait(pe, "t2_ready", i + 1)
                for t in range(NT):
                    last = T.transpose(pd[0:TT, t * P:(t + 1) * P], t2[:, u, t * TT:(t + 1) * TT], ident[:])
                last.then_inc(S["t2t_ready"], 1)
                wait(pe, "seen_ready", (i + 1) * NT)
                for t in range(NT):
                    last = T.matmul(pb[0:TT, t * E:(t + 1) * E], t2[:, u, t * TT:(t + 1) * TT], wr_c[:], start=True, stop=True)
                last.then_inc(S["logit_ready"], 1)
                wait(pe, "chosen_ready", i + 1)
                T.matmul(pc[:, 0:(NT + 1) * E], before[0:TT, :], chosen[:, :], start=True, stop=False)
                for t in range(NT):
                    n_after = NT - t
                    last = T.matmul(pc[:, (t + 1) * E:(NT + 1) * E].rearrange("p (t e) -> p t e", e=E), ones[0:TT, :],
                                    chosen[:, t * E:(t + 1) * E].rearrange("p (k e) -> p k e", k=1).broadcast_to([TT, n_after, E]),
                                    start=False, stop=(t == NT - 1))
                last.then_inc(S["rank_ready"], 1)

            images(pe, body)

            turned = pa[:].bitcast(F16)
            pe.wait_ge(S["tables_ready"], 1)
            pe.wait_ge(S["b2_moved"], 32)
            pe.wait_ge(S["w_lo_ready"], 2 * E)

            def turn(t, n, u):
                wait(pe, "xrt_copied", t - 1)
                wait(pe, f"xr_loaded_{u}", 16 * n + 16)
                for part in range(2):
                    for s in range(2):
                        c0 = 2 * BANK * (u % 2) + (2 * part + s) * P
                        last = T.transpose(turned[:, c0:c0 + P], xr[:, u, s, part * P:(part + 1) * P], ident16[:])
                last.then_inc(S["xrt_ready"], 1)

            def hidden(t, n, u, expert):
                w0 = expert * HID
                hp = (pb, pc)[u % 2]
                wait(pe, "g_ready", FC * (t - 1))
                wait(pe, "xrt_copied", t + 1)
                for f in range(FC):
                    for m, (wp, xp) in enumerate(((0, 0), (0, 1), (1, 0))):
                        last = T.matmul(hp[:, f * TILE:(f + 1) * TILE], w1[:, wp, bass.ds(w0 + f * P, P)],
                                        xrt[:, u % 2, 2 * xp:2 * xp + 2, :].rearrange("p s k -> p (s k)"), start=(m == 0), stop=(m == 2))
                    last.then_inc(S["h_ready"], 1)

            def output(t, n, u, expert):
                w0, c0 = expert * HID, expert * P
                wait(pe, "y_copied", t - 1)
                wait(pe, "ghl_ready", 2 * t + 2)
                for s in range(2):
                    b0 = (u % 2) * BANK + s * P
                    dst = pd[:, b0:b0 + P]
                    T.matmul(dst, two_rows[:], b2[:, bass.ds(c0, P)], start=True, stop=False)
                    for f in range(FC):
                        for m, (wp, gp) in enumerate(((0, 0), (1, 0), (0, 1))):
                            last = T.matmul(dst, ghl[:, u % 2, gp, f * TILE + s * P:f * TILE + (s + 1) * P],
                                            w2[:, wp, bass.ds(w0 + f * P, P)], start=False, stop=(f == FC - 1 and m == 2))
                last.then_inc(S["y_ready"], 1)

            experts = table(mybir.EngineType.PE, tile_w, 0, 2, E - 1)
            turn(0, 0, 0)
            hidden(0, 0, 0, experts[0])
            turn(1, 0, 1)
            hidden(1, 0, 1, experts[1])
            turn(2, 0, 2)

            def group(t0, n, count):
                experts = table(mybir.EngineType.PE, tile_w, t0, count + 2, E - 1)
                for u in range(count):
                    t = t0 + u
                    if later(t, n, u, 3):
                        turn(*later(t, n, u, 3))
                    if later(t, n, u, 2):
                        hidden(*later(t, n, u, 2), experts[u + 2])
                    output(t, n, u, experts[u])

            tiles(pe, group)

            def turn_sum(i, j, u):
                wait(pe, "o_ready", i - 1)
                wait(pe, "ysum_ready", i + 1)
                for t in range(NT):
                    last = T.transpose((pa, pb)[u][:, t * P:t * P + TT], ysum[:, u, t, :], ident[0:TT, 0:TT])
                last.then_inc(S["yt_ready"], 1)

            turn_sum(0, 0, 0)
            turn_sum(1, 0, 1)
            with pe.Fori(1, PAIRS) as j:
                turn_sum(2 * j, j, 0)
                turn_sum(2 * j + 1, j, 1)

        @block.scalar
        def _(act):
            A = nc.scalar
            act.wait_ge(S["pool_const"], POOL_CONSTS)

            def root(out_, in_, wait_name, wait_value, done_name):
                wait(act, wait_name, wait_value)
                A.activation(out_, in_, ACT.Sqrt).then_inc(S[done_name], 1)

            root(bn[:, :, 1], bn[:, :, 0], "bn_ln", 1, "bn_rstd")
            halves = pa[:, :].rearrange("p (h c) -> p h c", h=2)[:, :, 0:HALF]

            def s1_rstd(n):
                root(gs[:, 19:20], gs[:, 18:19], "gvar_ready", n + 1, "grstd_raw")

            def s1_norm(n, nu):
                wait(act, "gnorm_ready", n + 1)
                A.activation(padx[:, nu, 1:1 + SIDE, 1:1 + SIDE], xb[:, nu, :].rearrange("p (h w) -> p h w", w=SIDE),
                             ACT.Identity, scale=gs[:, 22:23], bias=gs[:, 23:24]).then_inc(S["xn_ready"], 1)

            def s1_h1(n):
                wait(act, "pw_ready", n)
                wait(act, "conv_ready", n + 1)
                A.activation(h1[:, :].rearrange("p (h c) -> p h c", h=2), halves, ACT.Relu,
                             scale=bn[:, 0, 6:7], bias=bn[:, 0, 7:8]).then_inc(S["h1_ready"], 1)

            def s1_h2(n):
                wait(act, "x1_ready", n)
                wait(act, "pw_ready", n + 1)
                A.activation(h2[:, :].rearrange("p (h c) -> p h c", h=2), halves, ACT.Relu,
                             scale=bn[:, 1, 6:7], bias=bn[:, 1, 7:8]).then_inc(S["h2_ready"], 1)

            act.wait_ge(S["consts_ready"], 1)
            s1_rstd(0)
            s1_norm(0, 0)
            s1_h1(0)
            s1_h2(0)

            def body(i, j, u, last_image):
                n, nu = i + 1, 1 - u
                root(ln[:, 0, 6, :], ln[:, 0, 5, :], "var1_ready", i + 1, "rstd1_raw")
                if not last_image:
                    s1_rstd(n)
                wait(act, "xnt_ready", i)
                wait(act, "norm1_ready", i + 1)
                for t in range(NT):
                    last = A.activation(xn[:, t, :], pb[0:TT, t * P:(t + 1) * P], ACT.Identity,
                                        scale=ln[:, 0, 1, t:t + 1], bias=ln[:, 0, 2, t:t + 1])
                last.then_inc(S["xn1_ready"], 1)
                if not last_image:
                    s1_norm(n, nu)
                    s1_h1(n)
                for t in range(NT):
                    if t == 0:
                        wait(act, "att_ready", i)
                    wait(act, "score_ready", i * NT + t + 1)
                    A.activation(seen[:, t * L + t * TT:(t + 1) * L], (pd, pb)[t % 2][0:TT, 0:L - t * TT], ACT.Sign).then_inc(S["seen_ready"], 1)
                if not last_image:
                    s1_h2(n)
                root(ln[:, 1, 6, :], ln[:, 1, 5, :], "var2_ready", i + 1, "rstd2_raw")
                wait(act, "rows_ready", i)
                wait(act, "norm2_ready", i + 1)
                for t in range(NT):
                    last = A.activation(xf[:, t, :], pd[0:TT, t * P:(t + 1) * P], ACT.Identity,
                                        scale=ln[:, 1, 1, t:t + 1], bias=ln[:, 1, 2, t:t + 1])
                last.then_inc(S["xn2_ready"], 1)
                wait(act, f"sent_{u}", 16 * 2 * NT * j)
                wait(act, "xn2_ready", i + 1)
                A.activation(rows[:, u, :, 0:P], xf[:, :, :], ACT.Identity).then_inc(S["hi_ready"], 1)
                if u == 0:
                    wait(act, "stage_loaded", 32 * j + 32)
                    A.activation(w1[:, 0, bass.ds(j * HID, HID)], w_stage[:, 0, :], ACT.Copy, scale=WSCALE).then_inc(S["w_hi_ready"], 1)
                    A.activation(w2[:, 0, bass.ds(j * HID, HID)], w_stage[:, 1, :], ACT.Copy, scale=WSCALE).then_inc(S["w_hi_ready"], 1)

            images(act, body)

            turned = pa[:].bitcast(F16)
            act.wait_ge(S["tables_ready"], 1)

            def copy_turned(t, n, u):
                wait(act, "h_ready", FC * (t - 1))
                wait(act, "xrt_ready", t + 1)
                A.activation(xrt[:, u % 2, :, :].rearrange("p s k -> p (s k)"), turned[:, 2 * BANK * (u % 2):2 * BANK * (u % 2) + 4 * P],
                             ACT.Copy).then_inc(S["xrt_copied"], 1)

            def gelu(t, n, u, expert):
                c0 = expert * FC
                hp = (pb, pc)[u % 2]
                wait(act, "ghl_ready", 2 * (t - 1))
                for f in range(FC):
                    wait(act, "h_ready", FC * t + 2 * (f // 2) + 2)
                    A.activation(g[:, u % 2, f, :], hp[:, f * TILE:(f + 1) * TILE], ACT.Gelu, scale=1.0 / WSCALE,
                                 bias=b1[:, bass.ds(c0 + f, 1)]).then_inc(S["g_ready"], 1)

            def gate_tanh(t, n, u):
                wait(act, "arg_ready", t + 1)
                A.activation(small[:, u, 2, :], small[:, u, 1, :], ACT.Tanh).then_inc(S["tanh_ready"], 1)

            experts = table(mybir.EngineType.Activation, tile_w, 0, 2, E - 1)
            copy_turned(0, 0, 0)
            gelu(0, 0, 0, experts[0])
            copy_turned(1, 0, 1)
            gelu(1, 0, 1, experts[1])
            gate_tanh(0, 0, 0)
            copy_turned(2, 0, 2)

            def group(t0, n, count):
                experts = table(mybir.EngineType.Activation, tile_w, t0, count + 2, E - 1)
                for u in range(count):
                    t = t0 + u
                    if later(t, n, u, 3):
                        copy_turned(*later(t, n, u, 3))
                    if later(t, n, u, 1):
                        gate_tanh(*later(t, n, u, 1))
                    if later(t, n, u, 2):
                        gelu(*later(t, n, u, 2), experts[u + 2])

            tiles(act, group)

            with act.Fori(0, PAIRS) as j:
                for u in range(2):
                    i = 2 * j + u
                    act.wait_ge(S["o_ready"], i + 1)
                    act.dma_start(out_img[bass.ds(i, 1)].rearrange("a c l -> c (a l)"), o[:, u, :]).then_inc(S[f"out_{u}"], 16)
            act.wait_ge(S["out_0"], 16 * PAIRS)
            act.wait_ge(S["out_1"], 16 * PAIRS)

        @block.vector
        def _(dve):
            V = nc.vector

            class Chain:

                def __init__(self, name, base):
                    self.name, self.base, self.n = name, base, 0

                def __call__(self, ins):
                    ins.then_inc(S[self.name], 1)
                    self.n += 1
                    dve.wait_ge(S[self.name], self.base + self.n)

            def bc_last(ap, n):
                return ap.rearrange("p (t k) -> p t k", k=1).broadcast_to([ap.shape[0], ap.shape[1], n])

            def bc_mid(ap, n):
                return ap.rearrange("p (k e) -> p k e", k=1).broadcast_to([ap.shape[0], n, ap.shape[1]])

            def newton(link, r, v, t0, t1, out_):
                link(V.reciprocal(out_, r))
                link(V.scalar_tensor_tensor(out=t0, in0=out_, scalar=-0.5, in1=out_, op0=ALU.mult, op1=ALU.mult))
                link(V.tensor_tensor(t1, t0, v, ALU.mult))
                link(V.scalar_tensor_tensor(out=t0, in0=t1, scalar=0.5, in1=out_, op0=ALU.add, op1=ALU.mult))
                link(V.tensor_tensor(out_, out_, t0, ALU.add))

            dve.wait_ge(S["pool_const"], POOL_CONSTS)
            dve.wait_ge(S["w_loaded"], 16 * W_LOADS)
            link = Chain("dve_set", 0)
            chan_bn = chan[:, 2:10].rearrange("p (l k) -> p l k", l=2)
            V.tensor_scalar(bn[:, :, 0], chan_bn[:, :, 3], EPS, None, ALU.add).then_inc(S["bn_ln"], 1)
            link(V.tensor_scalar(b2_tmp[:, 0, :], b2_raw[:, :], WSCALE, None, ALU.mult))
            link(V.scalar_tensor_tensor(out=b2_tmp[:, 1, :], in0=b2_raw[:, :], scalar=WSCALE, in1=b2_tmp[:, 0, :], op0=ALU.mult, op1=ALU.subtract))
            assert link.n == SET_B2
            dve.wait_ge(S["bn_rstd"], 1)
            dve.wait_ge(S["bn_ln"], 1)
            newton(link, bn[:, :, 1], bn[:, :, 0], bn[:, :, 3], bn[:, :, 4], bn[:, :, 5])
            link(V.tensor_tensor(bn[:, :, 6], bn[:, :, 5], chan_bn[:, :, 0], ALU.mult))
            link(V.tensor_tensor(bn[:, :, 3], chan[:, 0:2], chan_bn[:, :, 2], ALU.subtract))
            link(V.tensor_tensor(bn[:, :, 4], bn[:, :, 3], bn[:, :, 6], ALU.mult))
            link(V.tensor_tensor(bn[:, :, 7], bn[:, :, 4], chan_bn[:, :, 1], ALU.add))
            dve.wait_ge(S["w_turned"], 3)
            V.tensor_copy(w_t[:, :, :].rearrange("p n c -> p (n c)"), pa[:, 0:4 * P]).then_inc(S["w_copied"], 1)
            V.tensor_copy(b1[:, :], pb[:, 0:E * FC]).then_inc(S["w_copied"], 1)
            V.tensor_tensor(wr_c[:, :], wr[:, :], pc[:, 0:E], ALU.subtract).then_inc(S["w_copied"], 1)
            for tap in range(TAPS):
                last = V.tensor_scalar(tap_diag[:, tap, :], ident[:], dw_w[:, tap:tap + 1], None, ALU.mult)
            last.then_inc(S["consts_ready"], 1)

            def s1_stats(link, n, nj, nu):
                wait(dve, f"x_loaded_{nu}", 16 * nj + 16)
                V.bn_stats(gst[:, 0:6], xb[:, nu, 0:HALF])
                link(V.bn_stats(gst[:, 6:12], xb[:, nu, HALF:L]))
                stats = gst[:, :].rearrange("p (q k) -> p k q", k=3)
                link(V.tensor_tensor(gs[:, 0:4], stats[:, 1], stats[:, 1], ALU.mult))
                V.tensor_reduce(gs[:, 8:9], stats[:, 1], AX.X, ALU.add)
                V.tensor_reduce(gs[:, 4:5], gs[:, 0:4], AX.X, ALU.add)
                link(V.tensor_reduce(gs[:, 5:6], stats[:, 2], AX.X, ALU.add))
                V.scalar_tensor_tensor(out=gs[:, 9:10], in0=gs[:, 4:5], scalar=float(L // 4), in1=gs[:, 5:6],
                                       op0=ALU.mult, op1=ALU.add).then_inc(S["gstat_ready"], 1)

            def s1_variance(link, n):
                wait(dve, "gmean_ready", n + 1)
                V.tensor_scalar(gs[:, 14:15], pa[:, 0:1], 0.25, None, ALU.mult)
                V.tensor_scalar(gs[:, 15:16], pa[:, 1:2], 1.0 / L, None, ALU.mult)
                link(V.tensor_scalar(gs[:, 16:17], pa[:, 0:1], -0.25, None, ALU.mult))
                link(V.scalar_tensor_tensor(out=gs[:, 17:18], in0=gs[:, 14:15], scalar=gs[:, 16:17], in1=gs[:, 15:16], op0=ALU.mult, op1=ALU.add))
                V.tensor_scalar(gs[:, 18:19], gs[:, 17:18], EPS, None, ALU.add).then_inc(S["gvar_ready"], 1)

            def s1_scale(link, n):
                wait(dve, "grstd_raw", n + 1)
                wait(dve, "gvar_ready", n + 1)
                newton(link, gs[:, 19:20], gs[:, 18:19], gs[:, 20:21], gs[:, 21:22], gs[:, 22:23])
                V.tensor_tensor(gs[:, 23:24], gs[:, 16:17], gs[:, 22:23], ALU.mult).then_inc(S["gnorm_ready"], 1)

            def s1_mask(link, n):
                wait(dve, "h1_ready", n + 1)
                wait(dve, "pw_ready", n)
                link(V.tensor_reduce(gs[:, 24:25], h1[:, :], AX.X, ALU.max))
                link(V.tensor_scalar(gs[:, 25:26], gs[:, 24:25], DW_THRESH, None, ALU.is_ge))
                V.tensor_scalar(pw_masked[:], w_t[:, 3, :], gs[:, 25:26], None, ALU.mult).then_inc(S["pwm_ready"], 1)

            def s1_add(link, n, nu):
                wait(dve, "h2_ready", n + 1)
                link(V.tensor_reduce(gs[:, 26:27], h2[:, :], AX.X, ALU.max))
                link(V.tensor_scalar(gs[:, 27:28], gs[:, 26:27], PW_THRESH, None, ALU.is_ge))
                V.scalar_tensor_tensor(out=x1[:, nu, :], in0=h2[:, :], scalar=gs[:, 27:28], in1=xb[:, nu, :],
                                       op0=ALU.mult, op1=ALU.add).then_inc(S["x1_ready"], 1)

            def ln_stats(link, w, pair, done):
                for t in range(NT):
                    last = V.bn_stats(st[:, w, 6 * t:6 * t + 6], pair[0:TT, t * P:(t + 1) * P])
                link(last)
                stats = st[:, w, :].rearrange("p (t k) -> p k t", k=6)
                V.tensor_tensor(ln[:, w, 0, :], stats[:, 1], stats[:, 4], ALU.add)
                V.tensor_tensor(ln[:, w, 2, :], stats[:, 2], stats[:, 5], ALU.add)
                link(V.tensor_tensor(ln[:, w, 1, :], stats[:, 1], stats[:, 4], ALU.subtract))
                link(V.tensor_tensor(ln[:, w, 3, :], ln[:, w, 1, :], ln[:, w, 1, :], ALU.mult))
                link(V.scalar_tensor_tensor(out=ln[:, w, 4, :], in0=ln[:, w, 3, :], scalar=P / 4.0, in1=ln[:, w, 2, :], op0=ALU.mult, op1=ALU.add))
                V.tensor_scalar(ln[:, w, 5, :], ln[:, w, 4, :], 1.0 / P, EPS, ALU.mult, ALU.add).then_inc(S[done], 1)

            def ln_scale(link, w, raw, var, value, done):
                wait(dve, raw, value)
                wait(dve, var, value)
                newton(link, ln[:, w, 6, :], ln[:, w, 5, :], ln[:, w, 3, :], ln[:, w, 4, :], ln[:, w, 1, :])
                V.scalar_tensor_tensor(out=ln[:, w, 2, :], in0=ln[:, w, 0, :], scalar=-0.5, in1=ln[:, w, 1, :],
                                       op0=ALU.mult, op1=ALU.mult).then_inc(S[done], 1)

            def rt3(k):
                return rt[:, k, :].rearrange("p (t e) -> p t e", e=E)

            def pick(link, values, best, out_mask):
                link(V.tensor_reduce(rs[:, best, :], rt3(values), AX.X, ALU.max))
                link(V.tensor_tensor(rt3(1), rt3(values), bc_last(rs[:, best, :], E), ALU.is_equal))
                link(V.tensor_tensor(rt3(2), rt3(1), bc_mid(descend[0:TT, :], NT), ALU.mult))
                link(V.tensor_reduce(rs[:, 3, :], rt3(2), AX.X, ALU.max))
                link(V.tensor_tensor(rt3(out_mask), rt3(2), bc_last(rs[:, 3, :], E), ALU.is_equal))

            def s2(link1, link, i, j, u, last_image):
                n, nu = i + 1, 1 - u
                nj = j + u
                if not last_image:
                    s1_stats(link1, n, nj, nu)
                wait(dve, "t1_ready", i + 1)
                ln_stats(link, 0, pb, "var1_ready")
                if not last_image:
                    s1_variance(link1, n)
                ln_scale(link, 0, "rstd1_raw", "var1_ready", i + 1, "norm1_ready")
                if not last_image:
                    s1_scale(link1, n)
                wait(dve, "xnt_ready", i + 1)
                V.tensor_copy(xt[:, :].rearrange("p (t k) -> p t k", k=TT), pc[:, 0:NT * P].rearrange("p (t k) -> p t k", k=P)[:, :, 0:TT]).then_inc(S["xt_ready"], 1)
                wait(dve, "q_ready", i + 1)
                V.tensor_scalar(sq[:, :], pd[:, 0:L], Q_THRESH, None, ALU.is_ge).then_inc(S["sq_ready"], 1)
                wait(dve, "k_ready", i + 1)
                V.tensor_scalar(sk[:, :], pb[:, 0:L], K_THRESH, None, ALU.is_ge).then_inc(S["sk_ready"], 1)
                wait(dve, "v_ready", i + 1)
                V.tensor_scalar(sv[:, :], pc[0:TT, 0:NT * P], V_THRESH, None, ALU.is_ge).then_inc(S["sv_ready"], 1)
                if not last_image:
                    s1_mask(link1, n)
                wait(dve, "seen_ready", NT * i + NT)
                diag = seen.rearrange("p (t k) -> p t k", k=L + TT)[:, :, 0:TT]
                V.tensor_tensor(diag, diag, bc_mid(causal[0:TT, :], NT), ALU.mult).then_inc(S["tri_ready"], 1)
                wait(dve, f"t2_kept_{u}", 16 * j)
                wait(dve, "att_ready", i + 1)
                wait(dve, "x1_ready", i + 1)
                V.tensor_tensor(t2[:, u, :].rearrange("p (h c) -> p h c", h=2), pc[:, :].rearrange("p (h c) -> p h c", h=2)[:, :, 0:HALF],
                                x1[:, u, :].rearrange("p (h c) -> p h c", h=2), ALU.add).then_inc(S["t2_ready"], 1)
                if not last_image:
                    s1_add(link1, n, nu)
                wait(dve, "t2t_ready", i + 1)
                ln_stats(link, 1, pd, "var2_ready")
                ln_scale(link, 1, "rstd2_raw", "var2_ready", i + 1, "norm2_ready")
                wait(dve, "norm2_ready", i + 1)
                wait(dve, "logit_ready", i + 1)
                V.tensor_tensor(rt3(0), pb[0:TT, 0:NT * E].rearrange("p (t e) -> p t e", e=E), bc_last(ln[:, 1, 1, :], E), ALU.mult).then_inc(S["logit_read"], 1)
                wait(dve, "logit_read", i + 1)
                pick(link, 0, 0, 4)
                link(V.scalar_tensor_tensor(out=rt[:, 5, :], in0=rt[:, 4, :], scalar=-3.0e38, in1=rt[:, 0, :], op0=ALU.mult, op1=ALU.add))
                pick(link, 5, 2, 6)
                V.tensor_tensor(chosen[:, 0:NT * E], rt[:, 4, :], rt[:, 6, :], ALU.add).then_inc(S["chosen_ready"], 1)
                wait(dve, f"sent_{u}", 16 * 2 * NT * j)
                fields = rows[:, u, :, 2 * P:ROW].bitcast(F32)
                V.tensor_scalar(fields[:, :, 0], token[:, :], 2.0, None, ALU.mult)
                V.tensor_scalar(fields[:, :, 1], rs[:, 3, :], -1.0, float(E), ALU.mult, ALU.add)
                V.tensor_tensor(fields[:, :, 2], rs[:, 2, :], rs[:, 0, :], ALU.subtract)
                link(V.tensor_scalar(token[:, :], token[:, :], float(L), None, ALU.add))
                wait(dve, "hi_ready", i + 1)
                V.tensor_tensor(rows[:, u, :, P:2 * P], xf[:, :, :], rows[:, u, :, 0:P], ALU.subtract)
                wait(dve, "rank_ready", i + 1)
                link(V.tensor_tensor(rt3(7), pc[0:TT, 0:NT * E].rearrange("p (t e) -> p t e", e=E), bc_mid(base[0:TT, :], NT), ALU.add))
                V.tensor_tensor(base[:, :], base[:, :], pc[:, NT * E:(NT + 1) * E], ALU.add).then_inc(S["rank_read"], 1)
                wait(dve, "rank_read", i + 1)
                V.tensor_tensor(rt3(8), rt3(4), rt3(7), ALU.mult)
                link(V.tensor_tensor(rt3(9), rt3(6), rt3(7), ALU.mult))
                V.tensor_reduce(rs[:, 10, :], rt3(8), AX.X, ALU.add)
                link(V.tensor_reduce(rs[:, 11, :], rt3(9), AX.X, ALU.add))
                V.tensor_copy(pos[:, u, :, :].rearrange("p t k -> p k t"), rs[:, 10:12, :]).then_inc(S["rows_ready"], 1)
                if u == 0:
                    wait(dve, "w_hi_ready", 2 * j + 2)
                    for w, stage in ((w1, 0), (w2, 1)):
                        V.scalar_tensor_tensor(out=w[:, 1, bass.ds(j * HID, HID)], in0=w_stage[:, stage, :], scalar=WSCALE,
                                               in1=w[:, 0, bass.ds(j * HID, HID)], op0=ALU.mult, op1=ALU.subtract).then_inc(S["w_lo_ready"], 1)

            def body(i, j, u, last_image):
                link1, link2 = Chain("dve_s1", DVE_S1 * (i + 1)), Chain("dve_s2", DVE_S2 * i)
                s2(link1, link2, i, j, u, last_image)
                assert link1.n in (0, DVE_S1) and link2.n == DVE_S2, (link1.n, link2.n)

            first = Chain("dve_s1", 0)
            s1_stats(first, 0, 0, 0)
            s1_variance(first, 0)
            s1_scale(first, 0)
            s1_mask(first, 0)
            s1_add(first, 0, 0)
            assert first.n == DVE_S1, first.n
            images(dve, body)

            link = Chain("dve_tab", 0)
            link(V.scalar_tensor_tensor(out=tsmall[:, 0, :], in0=descend[:, :], scalar=float(REGION), in1=base[:, :], op0=ALU.mult, op1=ALU.add))
            link(V.tensor_scalar(tsmall[:, 1, :], tsmall[:, 0, :], -float(E * REGION), None, ALU.add))
            link(V.tensor_tensor(tcount[:, :, :], bc_last(tsmall[:, 1, :], MAXT), tcount[:, :, :], ALU.is_gt))
            link(V.tensor_reduce(tsmall[:, 2, :], tcount[:, :, :], AX.X, ALU.add))
            V.tensor_scalar(tsmall[:, 3, :], tsmall[:, 2, :], -float(TILE), float(REGION), ALU.mult, ALU.add)
            link(V.tensor_copy(tsmall[:, 4, 0:1], tsmall[:, 2, 0:1]))
            for e in range(1, E):
                link(V.tensor_tensor(tsmall[:, 4, e:e + 1], tsmall[:, 4, e - 1:e], tsmall[:, 2, e:e + 1], ALU.add))
            ended = tbig[:, 0, :].rearrange("p (t e) -> p t e", e=E)
            skipped = tbig[:, 1, :].rearrange("p (t e) -> p t e", e=E)
            link(V.tensor_tensor(ended, bc_last(tile_no[:, :], E), bc_mid(tsmall[:, 4, :], TILES), ALU.is_ge))
            V.tensor_reduce(tile_expert[:, :], ended, AX.X, ALU.add)
            link(V.tensor_tensor(skipped, ended, bc_mid(tsmall[:, 3, :], TILES), ALU.mult))
            link(V.tensor_reduce(tcol[:, 0, :], skipped, AX.X, ALU.add))
            V.scalar_tensor_tensor(out=tile_row[:, :], in0=tile_no[:, :], scalar=float(TILE), in1=tcol[:, 0, :], op0=ALU.mult, op1=ALU.add)
            V.tensor_scalar(tile_w[:, :], tile_expert[:, :], float(E - 1), None, ALU.min)
            V.tensor_copy(pad_at[:, :], base[:, :]).then_inc(S["tables_ready"], 1)

            def fields(t, n, u):
                f = xr[:, u, :, 2 * P:ROW].bitcast(F32)
                wait(dve, f"stored_{u}", 32 * n)
                wait(dve, f"xr_loaded_{u}", 16 * n + 16)
                link = Chain("dve_b", t)
                link(V.tensor_scalar(small[:, u, 0, :], f[:, :, 1], tile_expert[:, bass.ds(t, 1)], None, ALU.is_equal))
                V.scalar_tensor_tensor(out=small[:, u, 1, :], in0=small[:, u, 0, :], scalar=0.5, in1=f[:, :, 2],
                                       op0=ALU.subtract, op1=ALU.mult).then_inc(S["arg_ready"], 1)
                V.tensor_tensor(dest[:, u, :], small[:, u, 0, :], f[:, :, 0], ALU.add).then_inc(S["dest_ready"], 1)

            def split(t, n, u):
                wait(dve, "y_ready", t - 1)
                for h in range(2):
                    wait(dve, "g_ready", FC * t + 2 * h + 2)
                    V.tensor_copy(ghl[:, u % 2, 0, h * 2 * TILE:(h + 1) * 2 * TILE], gv(u, h)).then_inc(S["g_hi_ready"], 1)
                for h in range(2):
                    wait(dve, "g_hi_ready", 2 * t + h + 1)
                    V.tensor_tensor(ghl[:, u % 2, 1, h * 2 * TILE:(h + 1) * 2 * TILE], gv(u, h),
                                    ghl[:, u % 2, 0, h * 2 * TILE:(h + 1) * 2 * TILE], ALU.subtract).then_inc(S["ghl_ready"], 1)

            def gv(u, h):
                return g[:, u % 2, 2 * h:2 * h + 2, :].rearrange("p f k -> p (f k)")

            def gate(t, n, u):
                wait(dve, "tanh_ready", t + 1)
                V.tensor_scalar(small[:, u, 3, :], small[:, u, 2, :], 0.5 / WSCALE, 0.5 / WSCALE, ALU.mult, ALU.add).then_inc(S["gate_ready"], 1)

            def gated(t, n, u):
                wait(dve, "y_ready", t + 1)
                wait(dve, "gate_ready", t + 1)
                b0 = (u % 2) * BANK
                V.tensor_tensor(y[:, u, :, :], pd[:, b0:b0 + 2 * P].rearrange("p (s c) -> p s c", s=2),
                                bc_last(small[:, u, 3, :], P), ALU.mult).then_inc(S["y_copied"], 1)

            fields(0, 0, 0)
            fields(1, 0, 1)
            split(0, 0, 0)
            split(1, 0, 1)
            gate(0, 0, 0)

            def group(t0, n, count):
                for u in range(count):
                    t = t0 + u
                    if later(t, n, u, 2):
                        fields(*later(t, n, u, 2))
                    if later(t, n, u, 1):
                        gate(*later(t, n, u, 1))
                    gated(t, n, u)
                    if later(t, n, u, 2):
                        split(*later(t, n, u, 2))

            tiles(dve, group)

            def sum_rows(i, j, u):
                wait(dve, "yt_ready", i - 1)
                wait(dve, f"yl_loaded_{u}", 16 * j + 16)
                V.tensor_tensor(ysum[:, u, :, :], yl[:, u, :, 0, :], yl[:, u, :, 1, :], ALU.add).then_inc(S["ysum_ready"], 1)

            def add_rows(i, j, u):
                wait(dve, "yt_ready", i + 1)
                wait(dve, f"out_{u}", 16 * j)
                V.tensor_tensor(o[:, u, :].rearrange("p (t k) -> p t k", k=TT), (pa, pb)[u][:, 0:NT * P].rearrange("p (t k) -> p t k", k=P)[:, :, 0:TT],
                                t2_all[:, bass.ds(i * L, L)].rearrange("p (t k) -> p t k", k=TT), ALU.add).then_inc(S["o_ready"], 1)

            dve.wait_ge(S["t2_kept_0"], 16 * PAIRS)
            dve.wait_ge(S["t2_kept_1"], 16 * PAIRS)
            sum_rows(0, 0, 0)
            sum_rows(1, 0, 1)
            add_rows(0, 0, 0)
            add_rows(1, 0, 1)
            with dve.Fori(1, PAIRS) as j:
                sum_rows(2 * j, j, 0)
                sum_rows(2 * j + 1, j, 1)
                add_rows(2 * j, j, 0)
                add_rows(2 * j + 1, j, 1)


_INS = ["x"] + ["L0_conv_" + n for n in ("dw_w", "dw_b", "bn1_g", "bn1_b", "bn1_m", "bn1_v", "pw_w", "pw_b", "bn2_g", "bn2_b", "bn2_m", "bn2_v")] \
    + ["L1_attn_" + n for n in ("Wq", "Wk", "Wv")] + ["L1_ffn_" + n for n in ("Wr", "W1", "b1", "W2", "b2")]


def kernel(**inputs):
    import numpy as _np
    import concourse.bacc as _bacc
    from concourse import mybir as _mybir
    from concourse.bass_utils import run_bass_kernel_spmd as _run

    nc = _bacc.Bacc("TRN2", target_bir_lowering=False, num_devices=1)
    arrays, args = {}, {}
    for name in _INS:
        v = _np.ascontiguousarray(inputs[name])
        arrays[f"in_{name}"] = v
        args[name] = nc.dram_tensor(f"in_{name}", v.shape, _mybir.dt.from_np(v.dtype), kind="ExternalInput").ap()
    shape = tuple(inputs["x"].shape)
    out = nc.dram_tensor("out_0", shape, _mybir.dt.float32, kind="ExternalOutput").ap()
    build(nc, args, out)
    r = _run(nc, [arrays], core_ids=[0])
    return r.results[0]["out_0"]
```

```python
from contextlib import ExitStack

import concourse.bass as bass
from concourse import mybir

F32 = mybir.dt.float32
F16 = mybir.dt.float16
BF16 = mybir.dt.bfloat16
I32 = mybir.dt.int32
U32 = mybir.dt.uint32
ALU = mybir.AluOpType
ACT = mybir.ActivationFunctionType
AX = mybir.AxisListType

P = 128
IMAGES, SIDE = 16, 28
L = SIDE * SIDE
HALF = L // 2
TOKENS = IMAGES * L
TT, NT = 112, 7
PAD = SIDE + 2
TAPS = 9
EPS = 1e-5
GROUP = 4
DW_THRESH, PW_THRESH = 4.0, 0.001
Q_THRESH, K_THRESH, V_THRESH = 0.25, 0.25, 0.3
E, HID = 8, 512
FC = HID // P
WSCALE = 64.0
TILE = 256
REGION = TOKENS + TILE
TILES = (2 * TOKENS + E * (TILE - 1)) // TILE
LEAST_TILES = 2 * TOKENS // TILE
XROWS = E * REGION + (TILES - LEAST_TILES + 1) * TILE
ROW = 2 * P + 6
SKIP = 1.0e6
MAXT = TOKENS // TILE + 1
BANK = 512
DEEP = 4
LOOP_END = (TILES - 3) // DEEP
POOL_CONSTS = 25
W_LOADS = 18
CHANNEL_PARAMETERS = ("dw_b", "pw_b", "bn1_g", "bn1_b", "bn1_m", "bn1_v", "bn2_g", "bn2_b", "bn2_m", "bn2_v")
GN = 2 * NT
LOGITS = NT * P
NORMS = 2 * NT + 1
STEPS = IMAGES + 4
LOOP_FROM, LOOP_TO = 6, IMAGES - 2
SUM_PARTS = 7
DVE_STEPS = {"x": 4, "norm": 7, "z": 16}


def build(nc, a, out):
    xs = nc.dram_tensor("dispatched_rows", (XROWS, ROW // 2), U32, kind="Internal").ap()
    ys = nc.dram_tensor("expert_rows", (2 * TOKENS, P), F32, kind="Internal").ap()
    x_img = a["x"].rearrange("b c h w -> b c (h w)")
    out_img = out.rearrange("b c h w -> b c (h w)")

    with ExitStack() as ctx:
        def sb(name, shape, dt):
            return ctx.enter_context(nc.sbuf_tensor(name, shape, dt))

        def sem(name):
            return ctx.enter_context(nc.semaphore(name))

        psum = [ctx.enter_context(nc.psum_tensor(f"pair_{n}", [P, 2 * BANK], F32)) for n in "abcd"]
        pa, pb, pc, pd = psum

        ident = sb("ident", [P, P], F32)
        ident16 = sb("ident16", [P, P], F16)
        group_avg = sb("group_avg", [P, P], F32)
        before = sb("before", [P, P], BF16)
        ones = sb("ones", [P, P], BF16)
        causal = sb("causal", [P, TT], BF16)
        w_raw = sb("w_raw", [P, 4, P], F32)
        w_t = sb("w_t", [P, 4, P], F32)
        chan = sb("chan", [P, 10], F32)
        dw_w = sb("dw_w", [P, TAPS], F32)
        dw64 = sb("dw64", [P, TAPS], F32)
        tap_diag = sb("tap_diag", [P, 2, TAPS, P], F16)
        bn = sb("bn", [P, 2, 8], F32)
        wr = sb("wr", [P, E], F32)
        wr_c = sb("wr_c", [P, E], F32)
        avg_all = sb("avg_all", [P, P], F32)
        w1 = sb("w1", [P, 2, E * HID], F16)
        w2 = sb("w2", [P, 2, E * HID], F16)
        w_stage = sb("w_stage", [P, 2, HID], F32)
        b1_raw = sb("b1_raw", [E * FC, P], F32)
        b1 = sb("b1", [P, E * FC], F32)
        b2_raw = sb("b2_raw", [1, E * P], F32)
        b2 = sb("b2", [P, E * P], F16)
        b2_tmp = sb("b2_tmp", [1, 2, E * P], F16)
        two_rows = sb("two_rows", [P, P], F16)

        xb_x1 = sb("xb_x1", [P, 4 * L], F32)
        xb = xb_x1[:, 0:2 * L].rearrange("p (u l) -> p u l", u=2)
        x1 = xb_x1[:, 2 * L:4 * L].rearrange("p (u l) -> p u l", u=2)
        xn64 = sb("xn64", [P, L], F32)
        padx = sb("padx", [P, 2, 2, PAD, PAD], F16)
        h1 = sb("h1", [P, L], F32)
        h2 = sb("h2", [P, L], F32)
        gs = sb("gs", [P, 32], F32)
        gst = sb("gst", [P, 12], F32)
        pw_masked = sb("pw_masked", [P, P], F32)
        st = sb("st", [TT, 2 * NT * 6], F32)
        ln = sb("ln", [TT, 5, 2 * NT], F32)
        var = sb("var", [P, NORMS], F32)
        root = sb("root", [P, NORMS], F32)
        newt = sb("newt", [P, 2, NORMS], F32)
        rstd = sb("rstd", [P, NORMS], F32)
        shift = sb("shift", [P, NORMS], F32)
        xn = sb("xn", [TT, NT, P], F32)
        xt = sb("xt", [P, L], F32)
        xf = sb("xf", [TT, NT, P], F32)
        sq = sb("sq", [P, L], BF16)
        sk = sb("sk", [P, L], BF16)
        sv = sb("sv", [TT, NT * P], BF16)
        seen_g = sb("seen_g", [P, NT * (L + TT)], BF16)
        seen = seen_g[0:TT, :]
        t2 = sb("t2", [P, 2, L], F32)
        t2_all = sb("t2_all", [P, IMAGES * L], F32)
        rows = sb("rows", [TT, 2, NT, ROW], F16)
        pos = sb("pos", [TT, 2, NT, 2], I32)
        rt = sb("rt", [TT, 12, NT * E], F32)
        rs = sb("rs", [TT, 12, NT], F32)
        chosen = sb("chosen", [TT, (NT + 1) * E], BF16)
        base = sb("base", [P, E], F32)
        descend = sb("descend", [P, E], F32)
        token = sb("token", [TT, NT], F32)

        tcount = sb("tcount", [P, E, MAXT], F32)
        tsmall = sb("tsmall", [P, 8, E], F32)
        tbig = sb("tbig", [P, 2, TILES * E], F32)
        tcol = sb("tcol", [P, 4, TILES], F32)
        tile_no = sb("tile_no", [P, TILES], F32)
        tile_row = sb("tile_row", [P, TILES], I32)
        tile_expert = sb("tile_expert", [P, TILES], F32)
        tile_w = sb("tile_w", [P, TILES], I32)
        pad_at = sb("pad_at", [P, E], I32)
        pad_rows = sb("pad_rows", [P, 2, ROW], F16)

        xr = sb("xr", [P, DEEP, 2, ROW], F16)
        xrt = sb("xrt", [P, 2, 4, P], F16)
        g = seen_g[:, 0:4 * FC * TILE].bitcast(F32).rearrange("p (u f k) -> p u f k", u=2, f=FC)
        ghl = xb_x1[:, 0:2 * FC * TILE].bitcast(F16).rearrange("p (u h k) -> p u h k", u=2, h=2)
        y = xb_x1[:, 2 * FC * TILE:2 * FC * TILE + DEEP * 2 * P].rearrange("p (u s c) -> p u s c", u=DEEP, s=2)
        small = sb("small", [P, DEEP, 4, 2], F32)
        dest = sb("dest", [P, DEEP, 2], I32)

        w1_place = w1[:, :, :].rearrange("p n c -> p (n c)").bitcast(F32)
        w2_place = w2[:, :, :].rearrange("p n c -> p (n c)").bitcast(F32)
        yl = w1_place[0:TT, 0:4 * NT * P].rearrange("p (u t k d) -> p u t k d", u=2, t=NT, k=2)
        ysum = w2_place[0:TT, 0:2 * NT * P].rearrange("p (u t d) -> p u t d", u=2, t=NT)
        o = w2_place[:, 2 * NT * P:2 * NT * P + 2 * L].rearrange("p (u l) -> p u l", u=2)

        S = {n: sem(n) for n in (
            "w_loaded", "pool_const", "w_turned", "w_copied", "consts_ready", "bn_var", "bn_root",
            "dve_taps", "taps_ready", "dve_set", "b2_split", "b2_moved",
            "x_loaded_0", "x_loaded_1", "again_0", "again_1", "gstat_ready", "gmean_ready", "gvar_ready", "xn_ready", "xhi_ready", "xlo_ready", "conv_ready",
            "h1_ready", "pwm_ready", "pw_ready", "h2_ready", "x1_ready",
            "stats1_ready", "stats2_ready", "var_ready", "root_ready", "norm_ready",
            "t1_ready", "xn1_ready", "xnt_ready", "xt_ready",
            "q_ready", "k_ready", "v_ready", "sq_ready", "sk_ready", "sv_ready",
            "score_ready", "seen_ready", "tri_ready", "att_ready", "t2_ready", "t2_kept_0", "t2_kept_1",
            "t2t_ready", "logit_read", "xn2_ready", "hi_ready", "lo_ready", "chosen_ready", "rank_ready", "rank_read",
            "rows_ready", "sent_0", "sent_1", "gates", "stage_loaded", "w_hi_ready", "w_lo_ready",
            "dve_w", "dve_x", "dve_norm", "dve_z", "dve_tab", "dve_b",
            "tables_ready", "pad_ready", "padded",
            "xr_loaded_0", "xr_loaded_1", "xr_loaded_2", "xr_loaded_3", "xrt_ready", "xrt_copied",
            "h_ready", "g_ready", "g_hi_ready", "ghl_ready", "arg_ready", "tanh_ready", "gate_ready",
            "dest_ready", "y_ready", "y_copied", "stored_0", "stored_1", "stored_2", "stored_3",
            "yl_loaded_0", "yl_loaded_1", "ysum_ready", "yt_ready", "o_ready", "out_0", "out_1",
        )}

        block = ctx.enter_context(nc.Block())
        PAIRS = IMAGES // 2

        def some(value):
            return not (isinstance(value, int) and value <= 0)

        class Step:

            def __init__(self, k, j, u):
                self.k, self.j, self.u = k, j, u

            def image(self, d):
                if isinstance(self.k, int) and not 0 <= self.k - d < IMAGES:
                    return None
                return self.k - d, self.j + (self.u - d) // 2, (self.u - d) % 2

        def steps(eng, body):
            for k in range(LOOP_FROM):
                body(Step(k, k // 2, k % 2))
            with eng.Fori(LOOP_FROM // 2, LOOP_TO // 2) as j:
                body(Step(2 * j, j, 0))
                body(Step(2 * j + 1, j, 1))
            for k in range(LOOP_TO, STEPS):
                body(Step(k, k // 2, k % 2))

        def tiles(eng, group):
            group(0, 0, DEEP)
            with eng.Fori(1, LOOP_END) as n:
                group(DEEP * n, n, DEEP)
            for t in range(DEEP * LOOP_END, TILES, DEEP):
                group(t, t // DEEP, min(DEEP, TILES - t))

        def table(engine, entries, t, count, most):
            if isinstance(t, int):
                count = min(count, TILES - t)
            return nc.values_load_multi_w_load_instructions(
                entries[0:1, bass.ds(t, count)], engines=[engine], min_val=0, max_val=most,
                skip_runtime_bounds_check_because="VectorE has bounded every entry of the tables")[1]

        def later(t, n, u, d):
            if isinstance(t, int) and t + d >= TILES:
                return None
            return t + d, n + (u + d) // DEEP, (u + d) % DEEP

        @block.sync
        def _(sp):
            sp.dma_start(xb[:, 0, :], x_img[0]).then_inc(S["x_loaded_0"], 16)
            with nc.allow_non_contiguous_dma(reason="small parameters"):
                for n, name in enumerate(("L1_attn_Wq", "L1_attn_Wk", "L1_attn_Wv")):
                    sp.dma_start(w_raw[:, n, :], a[name]).then_inc(S["w_loaded"], 16)
                sp.dma_start(w_raw[:, 3, :], a["L0_conv_pw_w"].rearrange("o c h w -> o (c h w)")).then_inc(S["w_loaded"], 16)
                sp.dma_start(dw_w[:, :], a["L0_conv_dw_w"].rearrange("c k h w -> c (k h w)")).then_inc(S["w_loaded"], 16)
                for n, name in list(enumerate(CHANNEL_PARAMETERS))[:5]:
                    sp.dma_start(chan[:, n:n + 1], a["L0_conv_" + name].rearrange("(c k) -> c k", k=1)).then_inc(S["w_loaded"], 16)
                sp.dma_start(wr[:, :], a["L1_ffn_Wr"]).then_inc(S["w_loaded"], 16)
                sp.dma_start(b1_raw[:, :], a["L1_ffn_b1"].rearrange("e (f p) -> (e f) p", p=P)).then_inc(S["w_loaded"], 16)
                sp.dma_start(b2_raw[:, :], a["L1_ffn_b2"].rearrange("(k e) d -> k (e d)", k=1)).then_inc(S["w_loaded"], 16)
            sp.dma_start(xb[:, 1, :], x_img[1]).then_inc(S["x_loaded_1"], 16)
            sp.dma_start(x1[:, 0, :], x_img[0]).then_inc(S["again_0"], 16)
            sp.dma_start(x1[:, 1, :], x_img[1]).then_inc(S["again_1"], 16)
            sp.wait_ge(S["pad_ready"], 3)
            spare = TILES - LEAST_TILES + 1
            for n in range(spare):
                r0 = E * REGION + n * TILE
                sp.dma_start(xs[r0:r0 + TILE, :].rearrange("(s p) c -> p s c", p=P), pad_rows[:, :, :].bitcast(U32)).then_inc(S["padded"], 16)

            def body(step):
                j = step.j
                if step.u == 0 and step.image(0):
                    if some(2 * j):
                        sp.wait_ge(S["w_lo_ready"], 2 * j)
                    sp.dma_start(w_stage[:, 0, :], a["L1_ffn_W1"][bass.ds(j, 1)].rearrange("a d h -> d (a h)")).then_inc(S["stage_loaded"], 16)
                    sp.dma_start(w_stage[:, 1, :].rearrange("p (f d) -> p f d", f=FC),
                                 a["L1_ffn_W2"][bass.ds(j, 1)].rearrange("a (f p) d -> p (a f) d", p=P)).then_inc(S["stage_loaded"], 16)
                if step.image(3):
                    i, _, u = step.image(3)
                    sp.wait_ge(S["t2_ready"], i + 1)
                    sp.dma_start(t2_all[:, bass.ds(i * L, L)], t2[:, u, :]).then_inc(S[f"t2_kept_{u}"], 16)
                    if not isinstance(i, int) or i + 2 < IMAGES:
                        sp.dma_start(x1[:, u, :], x_img[bass.ds(i + 2, 1)].rearrange("a c l -> c (a l)")).then_inc(S[f"again_{u}"], 16)
                if step.image(0) and (not isinstance(step.k, int) or step.k + 2 < IMAGES):
                    i, _, u = step.image(0)
                    sp.wait_ge(S["xn_ready"], i + 1)
                    sp.dma_start(xb[:, u, :], x_img[bass.ds(i + 2, 1)].rearrange("a c l -> c (a l)")).then_inc(S[f"x_loaded_{u}"], 16)

            steps(sp, body)

            sp.wait_ge(S["tables_ready"], 1)
            pads_at = table(mybir.EngineType.SP, pad_at, 0, E, XROWS - TILE)
            for e in range(E):
                sp.dma_start(xs[bass.ds(pads_at[e], TILE), :].rearrange("(s p) c -> p s c", p=P), pad_rows[:, :, :].bitcast(U32)).then_inc(S["padded"], 16)
            sp.wait_ge(S["b2_split"], 2)
            sp.dma_start(b2[0:1, :], b2_tmp[:, 0, :]).then_inc(S["b2_moved"], 16)
            sp.dma_start(b2[1:2, :], b2_tmp[:, 1, :]).then_inc(S["b2_moved"], 16)
            sp.wait_ge(S["sent_0"], 16 * 2 * NT * PAIRS)
            sp.wait_ge(S["sent_1"], 16 * 2 * NT * PAIRS)
            if some(16 * (E + spare)):
                sp.wait_ge(S["padded"], 16 * (E + spare))

            def load_tiles(t0, n, count):
                rows_at = table(mybir.EngineType.SP, tile_row, t0, count, XROWS - TILE)
                for u in range(count):
                    t = t0 + u
                    if some(t - 3):
                        sp.wait_ge(S["xrt_ready"], t - 3)
                    if some(t - 3):
                        sp.wait_ge(S["dest_ready"], t - 3)
                    sp.wait_ge(S["tables_ready"], 1)
                    sp.dma_start(xr[:, u, :, :].bitcast(U32), xs[bass.ds(rows_at[u], TILE), :].rearrange("(s p) c -> p s c", p=P)).then_inc(S[f"xr_loaded_{u}"], 16)

            tiles(sp, load_tiles)

            for u in range(DEEP):
                if some(32 * ((TILES - u + DEEP - 1) // DEEP)):
                    sp.wait_ge(S[f"stored_{u}"], 32 * ((TILES - u + DEEP - 1) // DEEP))
            y_img = ys.rearrange("(b t p k) d -> b p t (k d)", b=IMAGES, t=NT, k=2)

            def load_y(i, j, u):
                if some(i - 1):
                    sp.wait_ge(S["ysum_ready"], i - 1)
                sp.dma_start(yl[:, u, :, :, :].rearrange("p t k d -> p t (k d)"),
                             y_img[bass.ds(i, 1)].rearrange("a p t d -> p (a t) d")).then_inc(S[f"yl_loaded_{u}"], 16)

            load_y(0, 0, 0)
            load_y(1, 0, 1)
            with sp.Fori(1, PAIRS) as j:
                load_y(2 * j, j, 0)
                load_y(2 * j + 1, j, 1)

        @block.gpsimd
        def _(pool):
            G = nc.gpsimd
            done = [0]

            def const(ins):
                done[0] += 1
                ins.then_inc(S["pool_const"], 1)

            def settle():
                pool.wait_ge(S["pool_const"], done[0])

            const(G.memset(ident[:], 0.0))
            const(G.memset(ident16[:], 0.0))
            const(G.memset(group_avg[:], 1.0 / GROUP))
            const(G.memset(before[:], 1.0))
            const(G.memset(causal[:], 1.0))
            const(G.memset(ones[:], 1.0))
            const(G.memset(avg_all[:], 1.0 / P))
            const(G.memset(padx[:], 0.0))
            const(G.memset(two_rows[:], 1.0))
            const(G.memset(b2[:], 0.0))
            const(G.memset(chosen[:], 0.0))
            const(G.memset(st[:], 0.0))
            const(G.memset(var[:], 1.0))
            const(G.iota(base[:], [[REGION, E]], base=0, channel_multiplier=0, allow_small_or_imprecise_dtypes=True))
            const(G.iota(descend[:], [[-1, E]], base=E, channel_multiplier=0, allow_small_or_imprecise_dtypes=True))
            const(G.iota(token[:], [[TT, NT]], base=0, channel_multiplier=1, allow_small_or_imprecise_dtypes=True))
            settle()
            const(G.affine_select(out=ident[:], in_=ident[:], compare_op=ALU.not_equal, fill=1.0, base=0, pattern=[[-1, P]], channel_multiplier=1))
            const(G.affine_select(out=ident16[:], in_=ident16[:], compare_op=ALU.not_equal, fill=1.0, base=0, pattern=[[-1, P]], channel_multiplier=1))
            ga = group_avg[:].rearrange("p (g r) -> p g r", r=GROUP)
            const(G.affine_select(out=ga, in_=ga, compare_op=ALU.is_ge, fill=0.0, base=0, pattern=[[-GROUP, P // GROUP], [0, GROUP]], channel_multiplier=1))
            const(G.affine_select(out=before[:], in_=before[:], compare_op=ALU.is_gt, fill=0.0, base=0, pattern=[[1, P]], channel_multiplier=-1))
            const(G.affine_select(out=causal[:], in_=causal[:], compare_op=ALU.is_ge, fill=0.0, base=0, pattern=[[1, TT]], channel_multiplier=-1))
            const(G.affine_select(out=two_rows[:], in_=two_rows[:], compare_op=ALU.is_ge, fill=0.0, base=1, pattern=[[0, P]], channel_multiplier=-1))
            settle()
            const(G.affine_select(out=ga, in_=ga, compare_op=ALU.is_ge, fill=0.0, base=GROUP - 1, pattern=[[GROUP, P // GROUP], [0, GROUP]], channel_multiplier=-1))
            const(G.iota(tile_no[:], [[1, TILES]], base=0, channel_multiplier=0, allow_small_or_imprecise_dtypes=True))
            const(G.iota(tcount[:], [[0, E], [TILE, MAXT]], base=0, channel_multiplier=0, allow_small_or_imprecise_dtypes=True))
            settle()
            assert done[0] == POOL_CONSTS, done
            G.memset(pad_rows[:], 0.0).then_inc(S["pad_ready"], 1)
            pool.wait_ge(S["pad_ready"], 1)
            G.memset(pad_rows[:, :, 2 * P:2 * P + 2].bitcast(F32), SKIP).then_inc(S["pad_ready"], 1)
            pool.wait_ge(S["pad_ready"], 2)
            G.memset(pad_rows[:, :, 2 * P + 2:ROW].bitcast(F32), 0.0).then_inc(S["pad_ready"], 1)
            def gate(name, value):
                pool.wait_ge(S[name], value)
                pool.sem_inc(S["gates"], 1)

            rows_end = pool.to_reg(XROWS - 1)
            table_end = pool.to_reg(2 * TOKENS - 1)

            def body(step):
                if step.image(0):
                    i, _, u = step.image(0)
                    gate("xhi_ready", i + 1)
                    G.tensor_tensor(padx[:, 1, u, 1:1 + SIDE, 1:1 + SIDE], xn64[:, :].rearrange("p (h w) -> p h w", w=SIDE),
                                    padx[:, 0, u, 1:1 + SIDE, 1:1 + SIDE], ALU.subtract).then_inc(S["xlo_ready"], 1)
                if not step.image(4):
                    return
                i, j, u = step.image(4)
                pool.wait_ge(S["hi_ready"], i + 1)
                G.tensor_tensor(rows[:, u, :, P:2 * P], xf[:, :, :], rows[:, u, :, 0:P], ALU.subtract).then_inc(S["lo_ready"], 1)
                gate("lo_ready", i + 1)
                gate("rows_ready", i + 1)
                for t in range(NT):
                    for k in range(2):
                        pool.indirect_dma_start(
                            xs, bass.IndirectOffsetOnAxis(ap=pos[:, u, t, k:k + 1].bitcast(U32), axis=0),
                            rows[:, u, t, :].bitcast(U32), None, bounds_check=rows_end, oob_is_err=False).then_inc(S[f"sent_{u}"], 16)

            steps(pool, body)

            def store_tiles(t0, n, count):
                for u in range(count):
                    gate("y_copied", t0 + u + 1)
                    for s in range(2):
                        pool.indirect_dma_start(
                            ys, bass.IndirectOffsetOnAxis(ap=dest[:, u, s:s + 1].bitcast(U32), axis=0),
                            y[:, u, s, :], None, bounds_check=table_end, oob_is_err=False).then_inc(S[f"stored_{u}"], 16)

            tiles(pool, store_tiles)

        @block.tensor
        def _(pe):
            T = nc.tensor
            pe.wait_ge(S["pool_const"], POOL_CONSTS)
            pe.wait_ge(S["w_loaded"], 16 * W_LOADS)
            for n in range(4):
                last = T.transpose(pa[:, n * P:(n + 1) * P], w_raw[:, n, :], ident[:])
            last.then_inc(S["w_turned"], 1)
            T.transpose(pb[:, 0:E * FC], b1_raw[:, :], ident[0:E * FC, 0:E * FC]).then_inc(S["w_turned"], 1)
            T.matmul(pc[:, 0:E], avg_all[:], wr[:], start=True, stop=True).then_inc(S["w_turned"], 1)
            pe.wait_ge(S["w_copied"], 3)

            def group_mean(i):
                if some(i - 2):
                    pe.wait_ge(S["sk_ready"], i - 2)
                pe.wait_ge(S["gstat_ready"], i + 1)
                T.matmul(pc[:, 0:2], group_avg[:], gs[:, 8:10], start=True, stop=True).then_inc(S["gmean_ready"], 1)

            def conv(i, u, first, end):
                if first == 0:
                    if some(i):
                        pe.wait_ge(S["h2_ready"], i)
                    pe.wait_ge(S["taps_ready"], 1)
                    pe.wait_ge(S["xhi_ready"], i + 1)
                    pe.wait_ge(S["xlo_ready"], i + 1)
                for p in range(first, end):
                    tap, h = p // 2, p % 2
                    ky, kx = tap // 3, tap % 3
                    for m, (wp, xp) in enumerate(((0, 0), (0, 1), (1, 0))):
                        last = T.matmul(pa[:, h * BANK:h * BANK + HALF], tap_diag[:, wp, tap, :],
                                        padx[:, xp, u, ky + 14 * h:ky + 14 * h + 14, kx:kx + SIDE],
                                        start=(tap == 0 and m == 0), stop=(tap == TAPS - 1 and m == 2))
                if end == 2 * TAPS:
                    last.then_inc(S["conv_ready"], 1)

            def pointwise(i):
                pe.wait_ge(S["pwm_ready"], i + 1)
                pe.wait_ge(S["h1_ready"], i + 1)
                for h in range(2):
                    last = T.matmul(pa[:, h * BANK:h * BANK + HALF], pw_masked[:], h1[:, h * HALF:(h + 1) * HALF], start=True, stop=True)
                last.then_inc(S["pw_ready"], 1)

            def turn_x1(i, u):
                if some(NT * i - 1):
                    pe.wait_ge(S["seen_ready"], NT * i - 1)
                if some(i):
                    pe.wait_ge(S["xt_ready"], i)
                pe.wait_ge(S["x1_ready"], i + 1)
                for t in range(NT):
                    last = T.transpose(pb[0:TT, t * P:(t + 1) * P], x1[:, u, t * TT:(t + 1) * TT], ident[:])
                last.then_inc(S["t1_ready"], 1)

            def turn_xn(i):
                pe.wait_ge(S["xn1_ready"], i + 1)
                for t in range(NT):
                    last = T.transpose(pb[:, t * P:t * P + TT], xn[:, t, :], ident[0:TT, 0:TT])
                last.then_inc(S["xnt_ready"], 1)

            def project(i, w, ready):
                for c0, c1 in ((0, BANK), (BANK, L)):
                    last = T.matmul(pc[:, c0:c1], w_t[:, w, :], xt[:, c0:c1], start=True, stop=True)
                last.then_inc(S[ready], 1)

            def queries(step, i):
                if some(i):
                    pe.wait_ge(S["t2_ready"], i)
                if step.image(0):
                    pe.wait_ge(S["gvar_ready"], i + 3)
                pe.wait_ge(S["xt_ready"], i + 1)
                project(i, 0, "q_ready")

            def keys(i):
                pe.wait_ge(S["sq_ready"], i + 1)
                project(i, 1, "k_ready")

            def values(i):
                for t in range(NT):
                    last = T.matmul(pb[0:TT, t * P:(t + 1) * P], xt[:, t * TT:(t + 1) * TT], w_t[:, 2, :], start=True, stop=True)
                last.then_inc(S["v_ready"], 1)

            def scores(i, ts):
                for t in ts:
                    width = L - t * TT
                    if t == 0:
                        pe.wait_ge(S["sk_ready"], i + 1)
                        if some(i - 1):
                            pe.wait_ge(S["rank_read"], i - 1)
                    if t == 1:
                        pe.wait_ge(S["sv_ready"], i + 1)
                    if t >= 2:
                        pe.wait_ge(S["seen_ready"], i * NT + t - 1)
                    pair = (pd, pb)[t % 2]
                    for c0 in range(0, width, BANK):
                        c1 = min(c0 + BANK, width)
                        last = T.matmul(pair[0:TT, c0:c1], sk[:, t * TT:(t + 1) * TT], sq[:, t * TT + c0:t * TT + c1], start=True, stop=True)
                    last.then_inc(S["score_ready"], 1)

            def attend(step, i):
                pe.wait_ge(S["tri_ready"], i + 1)
                pe.wait_ge(S["sv_ready"], i + 1)
                pe.wait_ge(S["sk_ready"], i + 1)
                if step.image(0):
                    pe.wait_ge(S["gvar_ready"], i + 4)
                for h in range(2):
                    tiles = [t for t in range(NT) if t * TT < (h + 1) * HALF]
                    for t in tiles:
                        l0 = max(t * TT, h * HALF)
                        last = T.matmul(pc[:, h * BANK + l0 - h * HALF:h * BANK + HALF], sv[:, t * P:(t + 1) * P],
                                        seen[:, t * L + l0:t * L + (h + 1) * HALF], start=(t == 0), stop=(t == tiles[-1]))
                last.then_inc(S["att_ready"], 1)

            def turn_t2(i, u):
                scored = min(i + 2, IMAGES) if isinstance(i, int) else i + 2
                pe.wait_ge(S["seen_ready"], NT * scored)
                if some(i):
                    pe.wait_ge(S["rank_read"], i)
                pe.wait_ge(S["t2_ready"], i + 1)
                for t in range(NT):
                    T.transpose(pd[0:TT, t * P:(t + 1) * P], t2[:, u, t * TT:(t + 1) * TT], ident[:])
                for t in range(NT):
                    last = T.matmul(pd[0:TT, LOGITS + t * E:LOGITS + (t + 1) * E], t2[:, u, t * TT:(t + 1) * TT], wr_c[:], start=True, stop=True)
                last.then_inc(S["t2t_ready"], 1)

            def rank(i):
                pe.wait_ge(S["xn2_ready"], i + 1)
                pe.wait_ge(S["chosen_ready"], i + 1)
                T.matmul(pd[:, 0:(NT + 1) * E], before[0:TT, :], chosen[:, :], start=True, stop=False)
                for t in range(NT):
                    n_after = NT - t
                    last = T.matmul(pd[:, (t + 1) * E:(NT + 1) * E].rearrange("p (t e) -> p t e", e=E), ones[0:TT, :],
                                    chosen[:, t * E:(t + 1) * E].rearrange("p (k e) -> p k e", k=1).broadcast_to([TT, n_after, E]),
                                    start=False, stop=(t == NT - 1))
                last.then_inc(S["rank_ready"], 1)

            def body(step):
                norm, cnv, add, att, moe = (step.image(d) for d in range(5))
                if norm:
                    group_mean(norm[0])
                if att:
                    scores(att[0], (0, 1, 2))
                if cnv:
                    conv(cnv[0], cnv[2], 0, 1)
                if att:
                    scores(att[0], (3,))
                if cnv:
                    conv(cnv[0], cnv[2], 1, 2)
                if att:
                    scores(att[0], (4,))
                if cnv:
                    conv(cnv[0], cnv[2], 2, 3)
                if att:
                    scores(att[0], (5, 6))
                if add:
                    turn_x1(add[0], add[2])
                if moe:
                    turn_t2(moe[0], moe[2])
                if cnv:
                    conv(cnv[0], cnv[2], 3, 6)
                if att:
                    attend(step, att[0])
                if cnv:
                    conv(cnv[0], cnv[2], 6, 14)
                if add:
                    turn_xn(add[0])
                if cnv:
                    conv(cnv[0], cnv[2], 14, 18)
                if add:
                    queries(step, add[0])
                    values(add[0])
                    keys(add[0])
                if cnv:
                    pointwise(cnv[0])
                if moe:
                    rank(moe[0])

            steps(pe, body)

            turned = pa[:].bitcast(F16)
            pe.wait_ge(S["tables_ready"], 1)
            pe.wait_ge(S["b2_moved"], 32)
            pe.wait_ge(S["w_lo_ready"], 2 * E)

            def turn(t, n, u):
                if some(t - 1):
                    pe.wait_ge(S["xrt_copied"], t - 1)
                pe.wait_ge(S[f"xr_loaded_{u}"], 16 * n + 16)
                for part in range(2):
                    for s in range(2):
                        c0 = 2 * BANK * (u % 2) + (2 * part + s) * P
                        last = T.transpose(turned[:, c0:c0 + P], xr[:, u, s, part * P:(part + 1) * P], ident16[:])
                last.then_inc(S["xrt_ready"], 1)

            def hidden(t, n, u, expert):
                w0 = expert * HID
                hp = (pb, pc)[u % 2]
                if some(FC * (t - 1)):
                    pe.wait_ge(S["g_ready"], FC * (t - 1))
                pe.wait_ge(S["xrt_copied"], t + 1)
                for f in range(FC):
                    for m, (wp, xp) in enumerate(((0, 0), (0, 1), (1, 0))):
                        last = T.matmul(hp[:, f * TILE:(f + 1) * TILE], w1[:, wp, bass.ds(w0 + f * P, P)],
                                        xrt[:, u % 2, 2 * xp:2 * xp + 2, :].rearrange("p s k -> p (s k)"), start=(m == 0), stop=(m == 2))
                    last.then_inc(S["h_ready"], 1)

            def output(t, n, u, expert):
                w0, c0 = expert * HID, expert * P
                if some(t - 1):
                    pe.wait_ge(S["y_copied"], t - 1)
                pe.wait_ge(S["ghl_ready"], 2 * t + 2)
                for s in range(2):
                    b0 = (u % 2) * BANK + s * P
                    dst = pd[:, b0:b0 + P]
                    T.matmul(dst, two_rows[:], b2[:, bass.ds(c0, P)], start=True, stop=False)
                    for f in range(FC):
                        for m, (wp, gp) in enumerate(((0, 0), (1, 0), (0, 1))):
                            last = T.matmul(dst, ghl[:, u % 2, gp, f * TILE + s * P:f * TILE + (s + 1) * P],
                                            w2[:, wp, bass.ds(w0 + f * P, P)], start=False, stop=(f == FC - 1 and m == 2))
                last.then_inc(S["y_ready"], 1)

            experts = table(mybir.EngineType.PE, tile_w, 0, 2, E - 1)
            turn(0, 0, 0)
            hidden(0, 0, 0, experts[0])
            turn(1, 0, 1)
            hidden(1, 0, 1, experts[1])
            turn(2, 0, 2)

            def group(t0, n, count):
                experts = table(mybir.EngineType.PE, tile_w, t0, count + 2, E - 1)
                for u in range(count):
                    t = t0 + u
                    if later(t, n, u, 3):
                        turn(*later(t, n, u, 3))
                    if later(t, n, u, 2):
                        hidden(*later(t, n, u, 2), experts[u + 2])
                    output(t, n, u, experts[u])

            tiles(pe, group)

            def turn_sum(i, j, u):
                if some(i - 1):
                    pe.wait_ge(S["o_ready"], i - 1)
                pe.wait_ge(S["ysum_ready"], i + 1)
                for t in range(NT):
                    last = T.transpose((pa, pb)[u][:, t * P:t * P + TT], ysum[:, u, t, :], ident[0:TT, 0:TT])
                last.then_inc(S["yt_ready"], 1)

            turn_sum(0, 0, 0)
            turn_sum(1, 0, 1)
            with pe.Fori(1, PAIRS) as j:
                turn_sum(2 * j, j, 0)
                turn_sum(2 * j + 1, j, 1)

        @block.scalar
        def _(act):
            A = nc.scalar
            with nc.allow_non_contiguous_dma(reason="small parameters"):
                for n, name in list(enumerate(CHANNEL_PARAMETERS))[5:]:
                    act.dma_start(chan[:, n:n + 1], a["L0_conv_" + name].rearrange("(c k) -> c k", k=1)).then_inc(S["w_loaded"], 16)
            act.wait_ge(S["pool_const"], POOL_CONSTS)

            act.wait_ge(S["bn_var"], 1)
            A.activation(bn[:, :, 1], bn[:, :, 0], ACT.Sqrt).then_inc(S["bn_root"], 1)

            def halves(pair):
                return pair[:, :].rearrange("p (h c) -> p h c", h=2)[:, :, 0:HALF]

            act.wait_ge(S["consts_ready"], 1)

            def group_norm(i, u):
                if some(i):
                    act.wait_ge(S["xlo_ready"], i)
                A.activation(xn64[:, :], xb[:, u, :], ACT.Identity, scale=gs[:, 22:23], bias=shift[:, GN:GN + 1]).then_inc(S["xn_ready"], 1)
                if some(i - 1):
                    act.wait_ge(S["conv_ready"], i - 1)
                act.wait_ge(S["xn_ready"], i + 1)
                A.activation(padx[:, 0, u, 1:1 + SIDE, 1:1 + SIDE], xn64[:, :].rearrange("p (h w) -> p h w", w=SIDE),
                             ACT.Identity).then_inc(S["xhi_ready"], 1)

            def first_relu(i):
                if some(i):
                    act.wait_ge(S["pw_ready"], i)
                act.wait_ge(S["conv_ready"], i + 1)
                A.activation(h1[:, :].rearrange("p (h c) -> p h c", h=2), halves(pa), ACT.Relu,
                             scale=bn[:, 0, 2:3], bias=bn[:, 0, 7:8]).then_inc(S["h1_ready"], 1)

            def second_relu(i):
                if some(i):
                    act.wait_ge(S["x1_ready"], i)
                act.wait_ge(S["pw_ready"], i + 1)
                A.activation(h2[:, :].rearrange("p (h c) -> p h c", h=2), halves(pa), ACT.Relu,
                             scale=bn[:, 1, 6:7], bias=bn[:, 1, 7:8]).then_inc(S["h2_ready"], 1)

            def layer_norm(out_, pair, n0, done):
                for t in range(NT):
                    last = A.activation(out_[:, t, :], pair[0:TT, t * P:(t + 1) * P], ACT.Identity,
                                        scale=rstd[0:TT, n0 + t:n0 + t + 1], bias=shift[0:TT, n0 + t:n0 + t + 1])
                last.then_inc(S[done], 1)

            def copy_xt(i):
                if some(i):
                    act.wait_ge(S["v_ready"], i)
                act.wait_ge(S["xnt_ready"], i + 1)
                A.activation(xt[:, :].rearrange("p (t k) -> p t k", k=TT), pb[:, 0:NT * P].rearrange("p (t k) -> p t k", k=P)[:, :, 0:TT],
                             ACT.Copy).then_inc(S["xt_ready"], 1)

            def see(i):
                for t in range(NT):
                    if t == 0:
                        if some(i):
                            act.wait_ge(S["att_ready"], i)
                    act.wait_ge(S["score_ready"], i * NT + t + 1)
                    A.activation(seen[:, t * L + t * TT:(t + 1) * L], (pd, pb)[t % 2][0:TT, 0:L - t * TT], ACT.Sign).then_inc(S["seen_ready"], 1)

            def high_rows(i, j, u):
                if some(16 * 2 * NT * j):
                    act.wait_ge(S[f"sent_{u}"], 16 * 2 * NT * j)
                act.wait_ge(S["xn2_ready"], i + 1)
                A.activation(rows[:, u, :, 0:P], xf[:, :, :], ACT.Identity).then_inc(S["hi_ready"], 1)

            def high_weights(j):
                act.wait_ge(S["stage_loaded"], 32 * j + 32)
                A.activation(w1[:, 0, bass.ds(j * HID, HID)], w_stage[:, 0, :], ACT.Copy, scale=WSCALE).then_inc(S["w_hi_ready"], 1)
                A.activation(w2[:, 0, bass.ds(j * HID, HID)], w_stage[:, 1, :], ACT.Copy, scale=WSCALE).then_inc(S["w_hi_ready"], 1)

            def deviations(step):
                act.wait_ge(S["var_ready"], step.k + 1)
                A.activation(root[:, :], var[:, :], ACT.Sqrt).then_inc(S["root_ready"], 1)
                act.wait_ge(S["norm_ready"], step.k + 1)

            def body(step):
                norm, cnv, add, att, moe = (step.image(d) for d in range(5))
                if att:
                    see(att[0])
                if norm and step.u == 0:
                    high_weights(step.j)
                deviations(step)
                if add:
                    if some(add[0]):
                        act.wait_ge(S["xnt_ready"], add[0])
                    layer_norm(xn, pb, 0, "xn1_ready")
                if norm:
                    group_norm(norm[0], norm[2])
                if add:
                    copy_xt(add[0])
                if cnv:
                    first_relu(cnv[0])
                if moe:
                    if some(moe[0]):
                        act.wait_ge(S["lo_ready"], moe[0])
                    layer_norm(xf, pd, NT, "xn2_ready")
                    high_rows(*moe)
                if cnv:
                    second_relu(cnv[0])

            steps(act, body)

            turned = pa[:].bitcast(F16)
            act.wait_ge(S["tables_ready"], 1)

            def copy_turned(t, n, u):
                if some(FC * (t - 1)):
                    act.wait_ge(S["h_ready"], FC * (t - 1))
                act.wait_ge(S["xrt_ready"], t + 1)
                A.activation(xrt[:, u % 2, :, :].rearrange("p s k -> p (s k)"), turned[:, 2 * BANK * (u % 2):2 * BANK * (u % 2) + 4 * P],
                             ACT.Copy).then_inc(S["xrt_copied"], 1)

            def gelu(t, n, u, expert):
                c0 = expert * FC
                hp = (pb, pc)[u % 2]
                if some(2 * (t - 1)):
                    act.wait_ge(S["ghl_ready"], 2 * (t - 1))
                for f in range(FC):
                    act.wait_ge(S["h_ready"], FC * t + 2 * (f // 2) + 2)
                    A.activation(g[:, u % 2, f, :], hp[:, f * TILE:(f + 1) * TILE], ACT.Gelu, scale=1.0 / WSCALE,
                                 bias=b1[:, bass.ds(c0 + f, 1)]).then_inc(S["g_ready"], 1)

            def gate_tanh(t, n, u):
                act.wait_ge(S["arg_ready"], t + 1)
                A.activation(small[:, u, 2, :], small[:, u, 1, :], ACT.Tanh).then_inc(S["tanh_ready"], 1)

            experts = table(mybir.EngineType.Activation, tile_w, 0, 2, E - 1)
            copy_turned(0, 0, 0)
            gelu(0, 0, 0, experts[0])
            copy_turned(1, 0, 1)
            gelu(1, 0, 1, experts[1])
            gate_tanh(0, 0, 0)
            copy_turned(2, 0, 2)

            def group(t0, n, count):
                experts = table(mybir.EngineType.Activation, tile_w, t0, count + 2, E - 1)
                for u in range(count):
                    t = t0 + u
                    if later(t, n, u, 3):
                        copy_turned(*later(t, n, u, 3))
                    if later(t, n, u, 1):
                        gate_tanh(*later(t, n, u, 1))
                    if later(t, n, u, 2):
                        gelu(*later(t, n, u, 2), experts[u + 2])

            tiles(act, group)

            with act.Fori(0, PAIRS) as j:
                for u in range(2):
                    i = 2 * j + u
                    act.wait_ge(S["o_ready"], i + 1)
                    act.dma_start(out_img[bass.ds(i, 1)].rearrange("a c l -> c (a l)"), o[:, u, :]).then_inc(S[f"out_{u}"], 16)
            act.wait_ge(S["out_0"], 16 * PAIRS)
            act.wait_ge(S["out_1"], 16 * PAIRS)

        @block.vector
        def _(dve):
            V = nc.vector

            class Chain:

                def __init__(self, name, base):
                    self.name, self.base, self.n = name, base, 0

                def __call__(self, ins, part=None, image=None):
                    ins.then_inc(S[self.name], 1)
                    self.n += 1
                    if part is not None:
                        group_sums(part, image)
                    dve.wait_ge(S[self.name], self.base + self.n)

            def bc_last(ap, n):
                return ap.rearrange("p (t k) -> p t k", k=1).broadcast_to([ap.shape[0], ap.shape[1], n])

            def bc_mid(ap, n):
                return ap.rearrange("p (k e) -> p k e", k=1).broadcast_to([ap.shape[0], n, ap.shape[1]])

            def newton(link, v, r, t0, t1, out_):
                link(V.reciprocal(out_, r))
                link(V.scalar_tensor_tensor(out=t0, in0=out_, scalar=-0.5, in1=out_, op0=ALU.mult, op1=ALU.mult))
                link(V.tensor_tensor(t1, t0, v, ALU.mult))
                link(V.scalar_tensor_tensor(out=out_, in0=t1, scalar=1.5, in1=out_, op0=ALU.add, op1=ALU.mult))

            dve.wait_ge(S["pool_const"], POOL_CONSTS)
            dve.wait_ge(S["w_loaded"], 16 * W_LOADS)
            link = Chain("dve_set", 0)
            chan_bn = chan[:, 2:10].rearrange("p (l k) -> p l k", l=2)
            V.tensor_scalar(bn[:, :, 0], chan_bn[:, :, 3], EPS, None, ALU.add).then_inc(S["bn_var"], 1)
            dve.wait_ge(S["bn_root"], 1)
            dve.wait_ge(S["bn_var"], 1)
            newton(link, bn[:, :, 0], bn[:, :, 1], bn[:, :, 3], bn[:, :, 4], bn[:, :, 5])
            link(V.tensor_tensor(bn[:, :, 6], bn[:, :, 5], chan_bn[:, :, 0], ALU.mult))
            link(V.tensor_tensor(bn[:, :, 3], chan[:, 0:2], chan_bn[:, :, 2], ALU.subtract))
            link(V.tensor_tensor(bn[:, :, 4], bn[:, :, 3], bn[:, :, 6], ALU.mult))
            link(V.tensor_tensor(bn[:, :, 7], bn[:, :, 4], chan_bn[:, :, 1], ALU.add))
            dve.wait_ge(S["w_turned"], 3)
            V.tensor_copy(w_t[:, :, :].rearrange("p n c -> p (n c)"), pa[:, 0:4 * P]).then_inc(S["w_copied"], 1)
            V.tensor_copy(b1[:, :], pb[:, 0:E * FC]).then_inc(S["w_copied"], 1)
            V.tensor_tensor(wr_c[:, :], wr[:, :], pc[:, 0:E], ALU.subtract).then_inc(S["w_copied"], 1)
            V.tensor_scalar(bn[:, 0, 2:3], bn[:, 0, 6:7], 1.0 / (WSCALE * WSCALE), None, ALU.mult).then_inc(S["consts_ready"], 1)

            def make_taps():
                link = Chain("dve_taps", 0)
                link(V.tensor_scalar(dw64[:, :], dw_w[:, :], WSCALE, None, ALU.mult))
                for tap in range(TAPS):
                    last = V.tensor_scalar(tap_diag[:, 0, tap, :], ident[:], dw64[:, tap:tap + 1], None, ALU.mult)
                link(last)
                for tap in range(TAPS):
                    last = V.scalar_tensor_tensor(out=tap_diag[:, 1, tap, :], in0=ident[:], scalar=dw64[:, tap:tap + 1],
                                                  in1=tap_diag[:, 0, tap, :], op0=ALU.mult, op1=ALU.subtract)
                last.then_inc(S["taps_ready"], 1)

            def group_sums(part, image):
                if not image:
                    return
                i, j, u = image
                stats = gst[:, :].rearrange("p (q k) -> p k q", k=3)
                if part == 0:
                    dve.wait_ge(S[f"x_loaded_{u}"], 16 * j + 16)
                    V.bn_stats(gst[:, 0:6], xb[:, u, 0:HALF])
                elif part == 1:
                    V.bn_stats(gst[:, 6:12], xb[:, u, HALF:L]).then_inc(S["dve_w"], 1)
                elif part == 2:
                    dve.wait_ge(S["dve_w"], 3 * i + 1)
                    V.tensor_tensor(gs[:, 0:4], stats[:, 1], stats[:, 1], ALU.mult).then_inc(S["dve_w"], 1)
                elif part == 3:
                    V.tensor_reduce(gs[:, 8:9], stats[:, 1], AX.X, ALU.add)
                elif part == 4:
                    dve.wait_ge(S["dve_w"], 3 * i + 2)
                    V.tensor_reduce(gs[:, 4:5], gs[:, 0:4], AX.X, ALU.add)
                elif part == 5:
                    V.tensor_reduce(gs[:, 5:6], stats[:, 2], AX.X, ALU.add).then_inc(S["dve_w"], 1)
                elif part == 6:
                    dve.wait_ge(S["dve_w"], 3 * i + 3)
                    V.scalar_tensor_tensor(out=gs[:, 9:10], in0=gs[:, 4:5], scalar=float(L // 4), in1=gs[:, 5:6],
                                           op0=ALU.mult, op1=ALU.add).then_inc(S["gstat_ready"], 1)

            def group_variance(i):
                dve.wait_ge(S["gmean_ready"], i + 1)
                V.tensor_scalar(gs[:, 14:15], pc[:, 0:1], 0.25, None, ALU.mult)
                V.tensor_scalar(gs[:, 15:16], pc[:, 1:2], 1.0 / L, EPS, ALU.mult, ALU.add)
                V.tensor_scalar(gs[:, 16:17], pc[:, 0:1], -0.25, None, ALU.mult).then_inc(S["gvar_ready"], 1)
                dve.wait_ge(S["gvar_ready"], i + 1)
                V.scalar_tensor_tensor(out=var[:, GN:GN + 1], in0=gs[:, 14:15], scalar=gs[:, 16:17], in1=gs[:, 15:16], op0=ALU.mult, op1=ALU.add)

            def token_stats(pair, n0, done):
                for t in range(NT):
                    last = V.bn_stats(st[:, 6 * (n0 + t):6 * (n0 + t) + 6], pair[0:TT, t * P:(t + 1) * P])
                last.then_inc(S[done], 1)

            def variances(link, step):
                if step.image(2):
                    dve.wait_ge(S["stats1_ready"], step.image(2)[0] + 1)
                if step.image(4):
                    dve.wait_ge(S["stats2_ready"], step.image(4)[0] + 1)
                stats = st[:, :].rearrange("p (t k) -> p k t", k=6)
                V.tensor_tensor(ln[:, 0, :], stats[:, 1], stats[:, 4], ALU.add)
                V.tensor_tensor(ln[:, 2, :], stats[:, 2], stats[:, 5], ALU.add)
                link(V.tensor_tensor(ln[:, 1, :], stats[:, 1], stats[:, 4], ALU.subtract))
                link(V.tensor_tensor(ln[:, 3, :], ln[:, 1, :], ln[:, 1, :], ALU.mult))
                link(V.scalar_tensor_tensor(out=ln[:, 4, :], in0=ln[:, 3, :], scalar=P / 4.0, in1=ln[:, 2, :], op0=ALU.mult, op1=ALU.add))
                V.tensor_scalar(var[0:TT, 0:GN], ln[:, 4, :], 1.0 / P, EPS, ALU.mult, ALU.add).then_inc(S["var_ready"], 1)

            def scales(link, step):
                dve.wait_ge(S["root_ready"], step.k + 1)
                dve.wait_ge(S["var_ready"], step.k + 1)
                newton(link, var[:, :], root[:, :], newt[:, 0, :], newt[:, 1, :], rstd[:, :])
                if step.image(0):
                    V.tensor_scalar(gs[:, 22:23], rstd[:, GN:GN + 1], WSCALE, None, ALU.mult)
                    V.scalar_tensor_tensor(out=shift[:, GN:GN + 1], in0=gs[:, 16:17], scalar=WSCALE, in1=rstd[:, GN:GN + 1],
                                           op0=ALU.mult, op1=ALU.mult)
                V.scalar_tensor_tensor(out=shift[0:TT, 0:GN], in0=ln[:, 0, :], scalar=-0.5, in1=rstd[0:TT, 0:GN],
                                       op0=ALU.mult, op1=ALU.mult).then_inc(S["norm_ready"], 1)

            def mask_weights(i):
                link = Chain("dve_x", DVE_STEPS["x"] * i)
                dve.wait_ge(S["h1_ready"], i + 1)
                if some(i):
                    dve.wait_ge(S["pw_ready"], i)
                link(V.tensor_reduce(gs[:, 24:25], h1[:, :], AX.X, ALU.max))
                link(V.tensor_scalar(gs[:, 25:26], gs[:, 24:25], DW_THRESH, None, ALU.is_ge))
                V.tensor_scalar(pw_masked[:], w_t[:, 3, :], gs[:, 25:26], None, ALU.mult).then_inc(S["pwm_ready"], 1)

            def add_block(i, j, u):
                link = Chain("dve_x", DVE_STEPS["x"] * i + 2)
                dve.wait_ge(S["h2_ready"], i + 1)
                link(V.tensor_reduce(gs[:, 26:27], h2[:, :], AX.X, ALU.max))
                link(V.tensor_scalar(gs[:, 27:28], gs[:, 26:27], PW_THRESH, None, ALU.is_ge))
                assert link.n + 2 == DVE_STEPS["x"], link.n
                dve.wait_ge(S[f"again_{u}"], 16 * j + 16)
                V.scalar_tensor_tensor(out=x1[:, u, :], in0=h2[:, :], scalar=gs[:, 27:28], in1=x1[:, u, :],
                                       op0=ALU.mult, op1=ALU.add).then_inc(S["x1_ready"], 1)

            def spikes(out_, in_, i, threshold, ready, done):
                dve.wait_ge(S[ready], i + 1)
                V.tensor_scalar(out_, in_, threshold, None, ALU.is_ge).then_inc(S[done], 1)

            def hide_later(i):
                if some(NT * i + NT):
                    dve.wait_ge(S["seen_ready"], NT * i + NT)
                diag = seen.rearrange("p (t k) -> p t k", k=L + TT)[:, :, 0:TT]
                V.tensor_tensor(diag, diag, bc_mid(causal[0:TT, :], NT), ALU.mult).then_inc(S["tri_ready"], 1)

            def add_attention(i, j, u):
                if some(16 * j):
                    dve.wait_ge(S[f"t2_kept_{u}"], 16 * j)
                dve.wait_ge(S["att_ready"], i + 1)
                dve.wait_ge(S["x1_ready"], i + 1)
                V.tensor_tensor(t2[:, u, :].rearrange("p (h c) -> p h c", h=2), pc[:, :].rearrange("p (h c) -> p h c", h=2)[:, :, 0:HALF],
                                x1[:, u, :].rearrange("p (h c) -> p h c", h=2), ALU.add).then_inc(S["t2_ready"], 1)

            def rt3(k):
                return rt[:, k, :].rearrange("p (t e) -> p t e", e=E)

            def pick(link, values, best, out_mask, parts, image):
                link(V.tensor_reduce(rs[:, best, :], rt3(values), AX.X, ALU.max), parts[0], image)
                link(V.tensor_tensor(rt3(1), rt3(values), bc_last(rs[:, best, :], E), ALU.is_equal), parts[1], image)
                link(V.tensor_tensor(rt3(2), rt3(1), bc_mid(descend[0:TT, :], NT), ALU.mult), parts[2], image)
                link(V.tensor_reduce(rs[:, 3, :], rt3(2), AX.X, ALU.max), parts[3], image)
                link(V.tensor_tensor(rt3(out_mask), rt3(2), bc_last(rs[:, 3, :], E), ALU.is_equal), parts[4], image)

            def take_logits(i):
                V.tensor_copy(rt[:, 10, :], pd[0:TT, LOGITS:LOGITS + NT * E]).then_inc(S["logit_read"], 1)

            def route(i, j, u, following):
                link = Chain("dve_z", DVE_STEPS["z"] * i)
                dve.wait_ge(S["logit_read"], i + 1)
                dve.wait_ge(S["norm_ready"], i + 5)
                link(V.tensor_tensor(rt3(0), rt3(10), bc_last(rstd[0:TT, NT:2 * NT], E), ALU.mult), 0, following)
                pick(link, 0, 0, 4, (1, 2, 3, 4, 5), following)
                link(V.scalar_tensor_tensor(out=rt[:, 5, :], in0=rt[:, 4, :], scalar=-3.0e38, in1=rt[:, 0, :], op0=ALU.mult, op1=ALU.add), 6, following)
                pick(link, 5, 2, 6, (None,) * 5, None)
                V.tensor_tensor(chosen[:, 0:NT * E], rt[:, 4, :], rt[:, 6, :], ALU.add).then_inc(S["chosen_ready"], 1)
                if some(16 * 2 * NT * j):
                    dve.wait_ge(S[f"sent_{u}"], 16 * 2 * NT * j)
                fields = rows[:, u, :, 2 * P:ROW].bitcast(F32)
                V.tensor_scalar(fields[:, :, 0], token[:, :], 2.0, None, ALU.mult)
                V.tensor_scalar(fields[:, :, 1], rs[:, 3, :], -1.0, float(E), ALU.mult, ALU.add)
                V.tensor_tensor(fields[:, :, 2], rs[:, 2, :], rs[:, 0, :], ALU.subtract)
                link(V.tensor_scalar(token[:, :], token[:, :], float(L), None, ALU.add))
                return link

            def place(link, i, u):
                dve.wait_ge(S["rank_ready"], i + 1)
                link(V.tensor_tensor(rt3(7), pd[0:TT, 0:NT * E].rearrange("p (t e) -> p t e", e=E), bc_mid(base[0:TT, :], NT), ALU.add))
                V.tensor_tensor(base[:, :], base[:, :], pd[:, NT * E:(NT + 1) * E], ALU.add).then_inc(S["rank_read"], 1)
                dve.wait_ge(S["rank_read"], i + 1)
                V.tensor_tensor(rt3(8), rt3(4), rt3(7), ALU.mult)
                link(V.tensor_tensor(rt3(9), rt3(6), rt3(7), ALU.mult))
                V.tensor_reduce(rs[:, 10, :], rt3(8), AX.X, ALU.add)
                link(V.tensor_reduce(rs[:, 11, :], rt3(9), AX.X, ALU.add))
                V.tensor_copy(pos[:, u, :, :].rearrange("p t k -> p k t"), rs[:, 10:12, :]).then_inc(S["rows_ready"], 1)
                assert link.n == DVE_STEPS["z"], link.n

            def low_weights(j):
                dve.wait_ge(S["w_hi_ready"], 2 * j + 2)
                for w, stage in ((w1, 0), (w2, 1)):
                    V.scalar_tensor_tensor(out=w[:, 1, bass.ds(j * HID, HID)], in0=w_stage[:, stage, :], scalar=WSCALE,
                                           in1=w[:, 0, bass.ds(j * HID, HID)], op0=ALU.mult, op1=ALU.subtract).then_inc(S["w_lo_ready"], 1)

            def body(step):
                norm, cnv, add, att, moe = (step.image(d) for d in range(5))
                following = step.image(-1) if not isinstance(step.k, int) or step.k + 1 < IMAGES else None
                norm_link = Chain("dve_norm", DVE_STEPS["norm"] * step.k)
                if norm:
                    group_variance(norm[0])
                if att:
                    hide_later(att[0])
                if add:
                    dve.wait_ge(S["t1_ready"], add[0] + 1)
                    token_stats(pb, 0, "stats1_ready")
                if moe:
                    dve.wait_ge(S["t2t_ready"], moe[0] + 1)
                    token_stats(pd, NT, "stats2_ready")
                    take_logits(moe[0])
                variances(norm_link, step)
                scales(norm_link, step)
                if att:
                    add_attention(*att)
                if norm and step.u == 1:
                    low_weights(step.j)
                if isinstance(step.k, int) and step.k == 0:
                    make_taps()
                if moe:
                    z_link = route(*moe, following)
                else:
                    for part in range(SUM_PARTS):
                        group_sums(part, following)
                if add:
                    spikes(sq[:, :], pc[:, 0:L], add[0], Q_THRESH, "q_ready", "sq_ready")
                if cnv:
                    mask_weights(cnv[0])
                if add:
                    spikes(sv[:, :], pb[0:TT, 0:NT * P], add[0], V_THRESH, "v_ready", "sv_ready")
                    spikes(sk[:, :], pc[:, 0:L], add[0], K_THRESH, "k_ready", "sk_ready")
                if moe:
                    place(z_link, moe[0], moe[2])
                if cnv:
                    add_block(*cnv)
                assert norm_link.n == DVE_STEPS["norm"], norm_link.n

            for part in range(SUM_PARTS):
                group_sums(part, (0, 0, 0))
            steps(dve, body)

            link = Chain("dve_tab", 0)
            link(V.scalar_tensor_tensor(out=tsmall[:, 0, :], in0=descend[:, :], scalar=float(REGION), in1=base[:, :], op0=ALU.mult, op1=ALU.add))
            link(V.tensor_scalar(tsmall[:, 1, :], tsmall[:, 0, :], -float(E * REGION), None, ALU.add))
            link(V.tensor_tensor(tcount[:, :, :], bc_last(tsmall[:, 1, :], MAXT), tcount[:, :, :], ALU.is_gt))
            link(V.tensor_reduce(tsmall[:, 2, :], tcount[:, :, :], AX.X, ALU.add))
            V.tensor_scalar(tsmall[:, 3, :], tsmall[:, 2, :], -float(TILE), float(REGION), ALU.mult, ALU.add)
            link(V.tensor_copy(tsmall[:, 4, 0:1], tsmall[:, 2, 0:1]))
            for e in range(1, E):
                link(V.tensor_tensor(tsmall[:, 4, e:e + 1], tsmall[:, 4, e - 1:e], tsmall[:, 2, e:e + 1], ALU.add))
            ended = tbig[:, 0, :].rearrange("p (t e) -> p t e", e=E)
            skipped = tbig[:, 1, :].rearrange("p (t e) -> p t e", e=E)
            link(V.tensor_tensor(ended, bc_last(tile_no[:, :], E), bc_mid(tsmall[:, 4, :], TILES), ALU.is_ge))
            V.tensor_reduce(tile_expert[:, :], ended, AX.X, ALU.add)
            link(V.tensor_tensor(skipped, ended, bc_mid(tsmall[:, 3, :], TILES), ALU.mult))
            link(V.tensor_reduce(tcol[:, 0, :], skipped, AX.X, ALU.add))
            V.scalar_tensor_tensor(out=tile_row[:, :], in0=tile_no[:, :], scalar=float(TILE), in1=tcol[:, 0, :], op0=ALU.mult, op1=ALU.add)
            V.tensor_scalar(tile_w[:, :], tile_expert[:, :], float(E - 1), None, ALU.min)
            V.tensor_copy(pad_at[:, :], base[:, :]).then_inc(S["tables_ready"], 1)

            link = Chain("b2_split", 0)
            link(V.tensor_scalar(b2_tmp[:, 0, :], b2_raw[:, :], WSCALE, None, ALU.mult))
            V.scalar_tensor_tensor(out=b2_tmp[:, 1, :], in0=b2_raw[:, :], scalar=WSCALE, in1=b2_tmp[:, 0, :],
                                   op0=ALU.mult, op1=ALU.subtract).then_inc(S["b2_split"], 1)

            def fields(t, n, u):
                f = xr[:, u, :, 2 * P:ROW].bitcast(F32)
                if some(32 * n):
                    dve.wait_ge(S[f"stored_{u}"], 32 * n)
                dve.wait_ge(S[f"xr_loaded_{u}"], 16 * n + 16)
                link = Chain("dve_b", t)
                link(V.tensor_scalar(small[:, u, 0, :], f[:, :, 1], tile_expert[:, bass.ds(t, 1)], None, ALU.is_equal))
                V.scalar_tensor_tensor(out=small[:, u, 1, :], in0=small[:, u, 0, :], scalar=0.5, in1=f[:, :, 2],
                                       op0=ALU.subtract, op1=ALU.mult).then_inc(S["arg_ready"], 1)
                V.tensor_tensor(dest[:, u, :], small[:, u, 0, :], f[:, :, 0], ALU.add).then_inc(S["dest_ready"], 1)

            def split(t, n, u):
                if some(t - 1):
                    dve.wait_ge(S["y_ready"], t - 1)
                for h in range(2):
                    dve.wait_ge(S["g_ready"], FC * t + 2 * h + 2)
                    V.tensor_copy(ghl[:, u % 2, 0, h * 2 * TILE:(h + 1) * 2 * TILE], gv(u, h)).then_inc(S["g_hi_ready"], 1)
                for h in range(2):
                    dve.wait_ge(S["g_hi_ready"], 2 * t + h + 1)
                    V.tensor_tensor(ghl[:, u % 2, 1, h * 2 * TILE:(h + 1) * 2 * TILE], gv(u, h),
                                    ghl[:, u % 2, 0, h * 2 * TILE:(h + 1) * 2 * TILE], ALU.subtract).then_inc(S["ghl_ready"], 1)

            def gv(u, h):
                return g[:, u % 2, 2 * h:2 * h + 2, :].rearrange("p f k -> p (f k)")

            def gate(t, n, u):
                dve.wait_ge(S["tanh_ready"], t + 1)
                V.tensor_scalar(small[:, u, 3, :], small[:, u, 2, :], 0.5 / WSCALE, 0.5 / WSCALE, ALU.mult, ALU.add).then_inc(S["gate_ready"], 1)

            def gated(t, n, u):
                dve.wait_ge(S["y_ready"], t + 1)
                dve.wait_ge(S["gate_ready"], t + 1)
                b0 = (u % 2) * BANK
                V.tensor_tensor(y[:, u, :, :], pd[:, b0:b0 + 2 * P].rearrange("p (s c) -> p s c", s=2),
                                bc_last(small[:, u, 3, :], P), ALU.mult).then_inc(S["y_copied"], 1)

            fields(0, 0, 0)
            fields(1, 0, 1)
            split(0, 0, 0)
            split(1, 0, 1)
            gate(0, 0, 0)

            def group(t0, n, count):
                for u in range(count):
                    t = t0 + u
                    if later(t, n, u, 2):
                        fields(*later(t, n, u, 2))
                    if later(t, n, u, 1):
                        gate(*later(t, n, u, 1))
                    gated(t, n, u)
                    if later(t, n, u, 2):
                        split(*later(t, n, u, 2))

            tiles(dve, group)

            def sum_rows(i, j, u):
                if some(i - 1):
                    dve.wait_ge(S["yt_ready"], i - 1)
                dve.wait_ge(S[f"yl_loaded_{u}"], 16 * j + 16)
                V.tensor_tensor(ysum[:, u, :, :], yl[:, u, :, 0, :], yl[:, u, :, 1, :], ALU.add).then_inc(S["ysum_ready"], 1)

            def add_rows(i, j, u):
                dve.wait_ge(S["yt_ready"], i + 1)
                if some(16 * j):
                    dve.wait_ge(S[f"out_{u}"], 16 * j)
                V.tensor_tensor(o[:, u, :].rearrange("p (t k) -> p t k", k=TT), (pa, pb)[u][:, 0:NT * P].rearrange("p (t k) -> p t k", k=P)[:, :, 0:TT],
                                t2_all[:, bass.ds(i * L, L)].rearrange("p (t k) -> p t k", k=TT), ALU.add).then_inc(S["o_ready"], 1)

            dve.wait_ge(S["t2_kept_0"], 16 * PAIRS)
            dve.wait_ge(S["t2_kept_1"], 16 * PAIRS)
            sum_rows(0, 0, 0)
            sum_rows(1, 0, 1)
            add_rows(0, 0, 0)
            add_rows(1, 0, 1)
            with dve.Fori(1, PAIRS) as j:
                sum_rows(2 * j, j, 0)
                sum_rows(2 * j + 1, j, 1)
                add_rows(2 * j, j, 0)
                add_rows(2 * j + 1, j, 1)


_INS = ["x"] + ["L0_conv_" + n for n in ("dw_w", "dw_b", "bn1_g", "bn1_b", "bn1_m", "bn1_v", "pw_w", "pw_b", "bn2_g", "bn2_b", "bn2_m", "bn2_v")] \
    + ["L1_attn_" + n for n in ("Wq", "Wk", "Wv")] + ["L1_ffn_" + n for n in ("Wr", "W1", "b1", "W2", "b2")]


def kernel(**inputs):
    import numpy as _np
    import concourse.bacc as _bacc
    from concourse import mybir as _mybir
    from concourse.bass_utils import run_bass_kernel_spmd as _run

    nc = _bacc.Bacc("TRN2", target_bir_lowering=False, num_devices=1)
    arrays, args = {}, {}
    for name in _INS:
        v = _np.ascontiguousarray(inputs[name])
        arrays[f"in_{name}"] = v
        args[name] = nc.dram_tensor(f"in_{name}", v.shape, _mybir.dt.from_np(v.dtype), kind="ExternalInput").ap()
    shape = tuple(inputs["x"].shape)
    out = nc.dram_tensor("out_0", shape, _mybir.dt.float32, kind="ExternalOutput").ap()
    build(nc, args, out)
    r = _run(nc, [arrays], core_ids=[0])
    return r.results[0]["out_0"]
```
